# Optimizing a Trainium2 kernel written in Bass

```python
import numpy as np
import jax
import jax.numpy as jnp

def _softmax(x, axis=-1):
    return jax.nn.softmax(x, axis=axis)
def _gelu(x):
    return jax.nn.gelu(x, approximate=True)
def _silu(x):
    return jax.nn.silu(x)
def _sigmoid(x):
    return jax.nn.sigmoid(x)
def _layernorm(x, axis=-1, eps=1e-5):
    m = jnp.mean(x, axis=axis, keepdims=True)
    v = jnp.var(x, axis=axis, keepdims=True)
    return (x - m) / jnp.sqrt(v + eps)
def _scatter_add(tgt, idx, src, axis=0):
    return tgt.at[idx].add(src)
def _segment_sum(src, seg, n):
    return jax.ops.segment_sum(src, seg, n)

kernel_name = 'mk_conv_seq_d1_conv_nchw128_1b53e5'

def setup_inputs(seed: int = 0):
    np.random.seed(seed)
    _w = jnp.asarray
    def _rec_inputs():
        import jax
        import jax.numpy as jnp
        _gk = jax.random.key(seed)
        x = 7.22e-05 + 1 * jax.random.normal(jax.random.fold_in(_gk, 1), (16, 128, 64, 64), jnp.float32)
        return x
    x = _rec_inputs()
    def _L0_conv_setup():
        import jax, jax.numpy as jnp
        import numpy as np
        B, DIM, H, W = (16, 128, 64, 64)
        D_INNER = 256
        D_STATE = 16
        DT_RANK = 16
        K = 2

        def _conv1x1(x, w, b):
            return jnp.einsum('bchw,oc->bohw', x, w) + b[None, :, None, None]

        def _ln_cf(x, w, b, eps=1e-06):
            m = x.mean(1, keepdims=True)
            v = ((x - m) ** 2).mean(1, keepdims=True)
            return (x - m) / jnp.sqrt(v + eps) * w[None, :, None, None] + b[None, :, None, None]

        def _silu(x):
            return x * jax.nn.sigmoid(x)

        def _ss2d_core(xi, x_proj_w, dt_proj_w, dt_proj_b, A_log, Ds):
            Bb, C, Hh, Ww = xi.shape
            L = Hh * Ww
            xf = xi.reshape(Bb, C, L)
            xs = jnp.stack([xf, xf[:, :, ::-1]], axis=1)
            x_dbl = jnp.einsum('bkcl,kdc->bkdl', xs, x_proj_w)
            dt, Bmat, Cmat = jnp.split(x_dbl, [DT_RANK, DT_RANK + D_STATE], axis=2)
            dt = jnp.einsum('bkrl,kcr->bkcl', dt, dt_proj_w) + dt_proj_b[None, :, :, None]
            dt = jax.nn.softplus(dt)
            A = -jnp.exp(A_log)
            x_l = jnp.moveaxis(xs, -1, 0)
            dt_l = jnp.moveaxis(dt, -1, 0)
            B_l = jnp.moveaxis(Bmat, -1, 0)
            C_l = jnp.moveaxis(Cmat, -1, 0)

            def step(hs, inp):
                x_t, dt_t, B_t, C_t = inp
                dA = jnp.exp(dt_t[..., None] * A[None])
                hs = hs * dA + (dt_t * x_t)[..., None] * B_t[:, :, None, :]
                y_t = jnp.einsum('bkcn,bkn->bkc', hs, C_t)
                return (hs, y_t)
            h0 = jnp.zeros((Bb, K, C, D_STATE), xi.dtype)
            _, ys = jax.lax.scan(step, h0, (x_l, dt_l, B_l, C_l))
            ys = jnp.moveaxis(ys, 0, -1) + Ds[None, :, :, None] * xs
            y = ys[:, 0] + ys[:, 1, :, ::-1]
            return y.reshape(Bb, C, Hh, Ww)
        key = jax.random.key(seed)
        ks = jax.random.split(key, 12)
        f = lambda i, shape, s=0.02: jax.random.normal(ks[i], shape, jnp.float32) * s
        return dict(x=jax.random.normal(ks[0], (B, DIM, H, W), jnp.float32), fc1_w=f(1, (D_INNER, DIM)), fc1_b=jnp.zeros((D_INNER,), jnp.float32), dw_w=f(2, (D_INNER, 1, 3, 3)), dw_b=jnp.zeros((D_INNER,), jnp.float32), in_proj_w=f(3, (2 * D_INNER, D_INNER)), in_proj_b=jnp.zeros((2 * D_INNER,), jnp.float32), x_proj_w=f(4, (K, DT_RANK + 2 * D_STATE, D_INNER)), dt_proj_w=f(5, (K, D_INNER, DT_RANK)), dt_proj_b=f(6, (K, D_INNER), 0.1), A_log=jnp.log(jnp.broadcast_to(jnp.arange(1, D_STATE + 1, dtype=jnp.float32), (K, D_INNER, D_STATE))), Ds=jnp.ones((K, D_INNER), jnp.float32), out_norm_w=jnp.ones((D_INNER,), jnp.float32), out_norm_b=jnp.zeros((D_INNER,), jnp.float32), out_proj_w=f(7, (D_INNER, D_INNER)), out_proj_b=jnp.zeros((D_INNER,), jnp.float32), norm_w=jnp.ones((D_INNER,), jnp.float32), norm_b=jnp.zeros((D_INNER,), jnp.float32), fc2_w=f(8, (DIM, D_INNER)), fc2_b=jnp.zeros((DIM,), jnp.float32))
    _L0_conv_all = _L0_conv_setup()
    _L0_conv_in = {k: v for k, v in _L0_conv_all.items() if k in ('fc1_w', 'fc1_b', 'dw_w', 'dw_b', 'in_proj_w', 'in_proj_b', 'x_proj_w', 'dt_proj_w', 'dt_proj_b', 'A_log', 'Ds', 'out_norm_w', 'out_norm_b', 'out_proj_w', 'out_proj_b', 'norm_w', 'norm_b', 'fc2_w', 'fc2_b', )}
    del _L0_conv_all

    return {
        "x": x,
        "L0_conv_fc1_w": _L0_conv_in["fc1_w"],
        "L0_conv_fc1_b": _L0_conv_in["fc1_b"],
        "L0_conv_dw_w": _L0_conv_in["dw_w"],
        "L0_conv_dw_b": _L0_conv_in["dw_b"],
        "L0_conv_in_proj_w": _L0_conv_in["in_proj_w"],
        "L0_conv_in_proj_b": _L0_conv_in["in_proj_b"],
        "L0_conv_x_proj_w": _L0_conv_in["x_proj_w"],
        "L0_conv_dt_proj_w": _L0_conv_in["dt_proj_w"],
        "L0_conv_dt_proj_b": _L0_conv_in["dt_proj_b"],
        "L0_conv_A_log": _L0_conv_in["A_log"],
        "L0_conv_Ds": _L0_conv_in["Ds"],
        "L0_conv_out_norm_w": _L0_conv_in["out_norm_w"],
        "L0_conv_out_norm_b": _L0_conv_in["out_norm_b"],
        "L0_conv_out_proj_w": _L0_conv_in["out_proj_w"],
        "L0_conv_out_proj_b": _L0_conv_in["out_proj_b"],
        "L0_conv_norm_w": _L0_conv_in["norm_w"],
        "L0_conv_norm_b": _L0_conv_in["norm_b"],
        "L0_conv_fc2_w": _L0_conv_in["fc2_w"],
        "L0_conv_fc2_b": _L0_conv_in["fc2_b"],
    }

def reference(x, L0_conv_fc1_w, L0_conv_fc1_b, L0_conv_dw_w, L0_conv_dw_b, L0_conv_in_proj_w, L0_conv_in_proj_b, L0_conv_x_proj_w, L0_conv_dt_proj_w, L0_conv_dt_proj_b, L0_conv_A_log, L0_conv_Ds, L0_conv_out_norm_w, L0_conv_out_norm_b, L0_conv_out_proj_w, L0_conv_out_proj_b, L0_conv_norm_w, L0_conv_norm_b, L0_conv_fc2_w, L0_conv_fc2_b):
    import jax
    import jax.numpy as jnp
    def _L0_conv_ref(x, fc1_w, fc1_b, dw_w, dw_b, in_proj_w, in_proj_b, x_proj_w, dt_proj_w, dt_proj_b, A_log, Ds, out_norm_w, out_norm_b, out_proj_w, out_proj_b, norm_w, norm_b, fc2_w, fc2_b):
        import jax, jax.numpy as jnp
        import numpy as np
        B, DIM, H, W = (16, 128, 64, 64)
        D_INNER = 256
        D_STATE = 16
        DT_RANK = 16
        K = 2

        def _conv1x1(x, w, b):
            return jnp.einsum('bchw,oc->bohw', x, w) + b[None, :, None, None]

        def _ln_cf(x, w, b, eps=1e-06):
            m = x.mean(1, keepdims=True)
            v = ((x - m) ** 2).mean(1, keepdims=True)
            return (x - m) / jnp.sqrt(v + eps) * w[None, :, None, None] + b[None, :, None, None]

        def _silu(x):
            return x * jax.nn.sigmoid(x)

        def _ss2d_core(xi, x_proj_w, dt_proj_w, dt_proj_b, A_log, Ds):
            Bb, C, Hh, Ww = xi.shape
            L = Hh * Ww
            xf = xi.reshape(Bb, C, L)
            xs = jnp.stack([xf, xf[:, :, ::-1]], axis=1)
            x_dbl = jnp.einsum('bkcl,kdc->bkdl', xs, x_proj_w)
            dt, Bmat, Cmat = jnp.split(x_dbl, [DT_RANK, DT_RANK + D_STATE], axis=2)
            dt = jnp.einsum('bkrl,kcr->bkcl', dt, dt_proj_w) + dt_proj_b[None, :, :, None]
            dt = jax.nn.softplus(dt)
            A = -jnp.exp(A_log)
            x_l = jnp.moveaxis(xs, -1, 0)
            dt_l = jnp.moveaxis(dt, -1, 0)
            B_l = jnp.moveaxis(Bmat, -1, 0)
            C_l = jnp.moveaxis(Cmat, -1, 0)

            def step(hs, inp):
                x_t, dt_t, B_t, C_t = inp
                dA = jnp.exp(dt_t[..., None] * A[None])
                hs = hs * dA + (dt_t * x_t)[..., None] * B_t[:, :, None, :]
                y_t = jnp.einsum('bkcn,bkn->bkc', hs, C_t)
                return (hs, y_t)
            h0 = jnp.zeros((Bb, K, C, D_STATE), xi.dtype)
            _, ys = jax.lax.scan(step, h0, (x_l, dt_l, B_l, C_l))
            ys = jnp.moveaxis(ys, 0, -1) + Ds[None, :, :, None] * xs
            y = ys[:, 0] + ys[:, 1, :, ::-1]
            return y.reshape(Bb, C, Hh, Ww)
        shortcut = x
        h = _conv1x1(x, fc1_w, fc1_b)
        h = jax.lax.conv_general_dilated(h, dw_w, (1, 1), 'SAME', dimension_numbers=('NCHW', 'OIHW', 'NCHW'), feature_group_count=h.shape[1]) + dw_b[None, :, None, None]
        h = _silu(h)
        xz = _conv1x1(h, in_proj_w, in_proj_b)
        xi, z = jnp.split(xz, 2, axis=1)
        xi = _silu(xi)
        y = _ss2d_core(xi, x_proj_w, dt_proj_w, dt_proj_b, A_log, Ds)
        y = _ln_cf(y, out_norm_w, out_norm_b)
        y = y * _silu(z)
        y = _conv1x1(y, out_proj_w, out_proj_b)
        y = _ln_cf(y, norm_w, norm_b)
        y = _conv1x1(y, fc2_w, fc2_b)
        return y + shortcut

    def _gn(v, G=32, eps=1e-5):
        B_, C_, H_, W_ = v.shape
        g = v.reshape(B_, G, C_ // G, H_, W_)
        m = jnp.mean(g, axis=(2, 3, 4), keepdims=True)
        s = jnp.var(g, axis=(2, 3, 4), keepdims=True)
        return ((g - m) / jnp.sqrt(s + eps)).reshape(v.shape)

    def _ln_c(v, eps=1e-6):
        m = jnp.mean(v, axis=1, keepdims=True)
        s = jnp.var(v, axis=1, keepdims=True)
        return (v - m) / jnp.sqrt(s + eps)

    def _ln_t(v, eps=1e-5):
        m = jnp.mean(v, axis=-1, keepdims=True)
        s = jnp.var(v, axis=-1, keepdims=True)
        return (v - m) / jnp.sqrt(s + eps)

    def _to_tokens(v):
        B_, C_, H_, W_ = v.shape
        return v.reshape(B_, C_, H_ * W_).transpose(0, 2, 1)
    def _from_tokens(t, like):
        B_, C_, H_, W_ = like.shape
        return t.transpose(0, 2, 1).reshape(B_, C_, H_, W_)

    x = _L0_conv_ref(x, L0_conv_fc1_w, L0_conv_fc1_b, L0_conv_dw_w, L0_conv_dw_b, L0_conv_in_proj_w, L0_conv_in_proj_b, L0_conv_x_proj_w, L0_conv_dt_proj_w, L0_conv_dt_proj_b, L0_conv_A_log, L0_conv_Ds, L0_conv_out_norm_w, L0_conv_out_norm_b, L0_conv_out_proj_w, L0_conv_out_proj_b, L0_conv_norm_w, L0_conv_norm_b, L0_conv_fc2_w, L0_conv_fc2_b)
    return x


_drawn_inputs = setup_inputs


def setup_inputs(seed=0):
    import zlib

    import numpy as np

    out = dict(_drawn_inputs(seed))
    spreads = {'L0_conv_fc1_b': (0.0, 0.8),
     'L0_conv_dw_b': (0.0, 0.669),
     'L0_conv_in_proj_b': (0.0, 0.1),
     'L0_conv_Ds': (1.0, 0.6),
     'L0_conv_out_norm_w': (1.0, 0.6),
     'L0_conv_out_norm_b': (0.0, 0.8),
     'L0_conv_out_proj_b': (0.0, 0.1),
     'L0_conv_norm_w': (1.0, 0.2),
     'L0_conv_norm_b': (0.0, 0.1),
     'L0_conv_fc2_b': (0.0, 0.1)}
    factors = {'L0_conv_fc1_w': 8.0,
     'L0_conv_dw_w': 8.0,
     'L0_conv_in_proj_w': 4.257,
     'L0_conv_x_proj_w': 8.0,
     'L0_conv_dt_proj_w': 8.0,
     'L0_conv_dt_proj_b': 8.0,
     'L0_conv_A_log': 8.0}
    for name, (base, spread) in spreads.items():
        noise = np.random.default_rng([zlib.crc32(name.encode()), seed]).standard_normal(out[name].shape)
        drawn = base * np.exp(spread * noise) if base else spread * noise
        out[name] = jnp.asarray(drawn.astype(out[name].dtype))
    for name, factor in factors.items():
        out[name] = (out[name] * factor).astype(out[name].dtype)
    return out
```

```python
from contextlib import ExitStack

import numpy as np

import concourse.bass as bass
from concourse import mybir

ALU = mybir.AluOpType
ACT = mybir.ActivationFunctionType
F32 = mybir.dt.float32
BF16 = mybir.dt.bfloat16

IMAGES, DIM, H, W = 16, 128, 64, 64
P = 128
INNER, STATES, RANK, DIRS = 256, 16, 16, 2
HALVES = INNER // P
TOKENS = H * W
WIN = 512
WINS = TOKENS // WIN
BLOCKS = WIN // P
HALF = WIN // 2
PRES = TOKENS // HALF
ROWS = HALF // W
STEPS = DIRS * WINS
TAPS = 9
PARTS = 3
SPREAD = PARTS * 2 * STATES
LOW = SPREAD + RANK
EPS = 1e-6
RING = 4
LAG = 2
EXP_CAP = 40.0
LN_EXP_SET = "natural_log_exp_and_others"
SILU_SET = "silu_and_others"


class Step:

    def __init__(self, b, k, w, parity, first_image, last_image):
        self.b, self.k, self.w, self.parity = b, k, w, parity
        self.s = b * STEPS + k * WINS + w
        self.static_w = w if isinstance(w, int) else None
        w0 = self.static_w
        self.first = first_image and k == 0 and w0 == 0
        self.last = last_image and k == 1 and w0 == WINS - 1
        self.pre = not last_image
        self.pre_index = (b + 1) * PRES + k * WINS + w
        if self.first:
            self.finish = False
        elif last_image:
            self.finish = k == 0 and w0 == 0
        else:
            self.finish = True
        if w0 == 0:
            self.left = None if self.first else (1 - k)
        else:
            self.left = k
        self.keep_y0 = self.left == 0
        self.keep_window = WINS - 1 if (k == 1 and w0 == 0) else w - 1
        self.kept_before = b * WINS + self.keep_window
        if k == 1:
            self.post1 = w0 is None or w0 >= 1
            self.post2 = w0 is None or w0 >= 2
            self.p1 = b * WINS + w - 1
            self.p2 = b * WINS + w - 2
            self.p1_window, self.p2_window = w * -1 + WINS, w * -1 + (WINS + 1)
        else:
            self.post1 = w0 == 0 and not first_image
            self.post2 = w0 in (0, 1) and not first_image
            self.p1 = b * WINS - 1
            self.p1_window = 0
            self.p2 = b * WINS - 2 + w
            self.p2_window = 1 - w if w0 in (0, 1) else 0
        self.post1_before = (k == 1 and (w0 is None or w0 >= 2)) or (k == 0 and w0 in (0, 1) and not first_image)
        self.p1_before = self.p2


def walk(engine, do_step):

    def image(b, first, last):
        for k in range(DIRS):
            head = WINS if first and k == 1 else 2
            for w in range(head):
                do_step(Step(b, k, w, w % 2, first, last))
            if head < WINS:
                with engine.Fori(1, WINS // 2 - 1) as j:
                    for par in range(2):
                        do_step(Step(b, k, 2 * j + par, par, first, last))
                for w in range(WINS - 2, WINS):
                    do_step(Step(b, k, w, w % 2, first, last))

    image(0, True, False)
    with engine.Fori(1, IMAGES - 1) as b:
        image(b, False, False)
    image(IMAGES - 1, False, True)


def blocks_of(window):
    if isinstance(window, int):
        return slice(window * BLOCKS, (window + 1) * BLOCKS)
    return bass.ds(window * BLOCKS, BLOCKS)


def wait(engine, sem, value):
    if isinstance(value, int) and value <= 0:
        return
    engine.wait_ge(sem, value)


def build(nc, d):
    ctx = ExitStack()
    with ctx:
        def sb(name, shape, dt=F32):
            return ctx.enter_context(nc.sbuf_tensor(name, shape, dt))

        def ps(name, shape):
            return ctx.enter_context(nc.psum_tensor(name, shape, F32))

        def sem(name):
            return ctx.enter_context(nc.semaphore(name))

        x_flat = d["x"].rearrange("b c h w -> b c (h w)")
        out_flat = d["out"].rearrange("b c h w -> b c (h w)")
        xi_dram = nc.dram_tensor("xi_scratch", (IMAGES, P, HALVES, TOKENS), F32, kind="Internal").ap()
        z_dram = nc.dram_tensor("z_scratch", (IMAGES, P, HALVES, TOKENS), F32, kind="Internal").ap()

        ident = sb("ident", [P, P])
        select = sb("select", [SPREAD, 2 * STATES, P], BF16)
        part_weight = sb("part_weight", [SPREAD, 2])
        conv_w = sb("conv_w", [P, TAPS, INNER])
        edge_w = sb("edge_w", [TAPS + 1, INNER])
        in_w = sb("in_w", [P, HALVES, 2 * INNER])
        in_b = sb("in_b", [1, 2 * INNER])
        ones = sb("ones", [1, HALF])
        low_w = sb("low_w", [P, HALVES, LOW])
        dt_w = sb("dt_w", [LOW, INNER])
        dt_b = sb("dt_b", [P, HALVES])
        A = sb("A", [P, DIRS, HALVES, STATES])
        D = sb("D", [P, DIRS, HALVES])
        D_sum = sb("D_sum", [P, HALVES])
        norm1_w = sb("norm1_w", [P, HALVES])
        norm1_b = sb("norm1_b", [P, HALVES])
        norm2_w = sb("norm2_w", [P, HALVES])
        norm2_b = sb("norm2_b", [P, HALVES])
        out_w = sb("out_w", [P, HALVES, INNER])
        out_b = sb("out_b", [1, INNER])
        fc2_w = sb("fc2_w", [P, HALVES, DIM])
        fc2_b = sb("fc2_b", [P, 1])
        minus_half = sb("minus_half", [P, BLOCKS])

        x_halo = sb("x_halo", [P, ROWS + 2, W + 2])
        edge_rows = sb("edge_rows", [TAPS + 1, HALF])
        hidden = sb("hidden", [P, HALVES, HALF])
        xi_out = sb("xi_out", [P, HALVES, HALF])
        z_out = sb("z_out", [P, HALVES, HALF])
        xi = [sb(f"xi{i}", [P, HALVES, WIN]) for i in range(2)]
        dt = [sb(f"dt{i}", [P, HALVES, WIN]) for i in range(2)]
        dtx = [sb(f"dtx{i}", [P, HALVES, WIN]) for i in range(2)]
        parts = [sb(f"parts{i}", [SPREAD, WIN], BF16) for i in range(2)]
        part_high = sb("part_high", [SPREAD, WIN], BF16)
        part_mid = sb("part_mid", [SPREAD, WIN], BF16)
        part_rest = sb("part_rest", [SPREAD, WIN])
        low_dt = sb("low_dt", [LOW, WIN])
        dt_lin = sb("dt_lin", [P, HALVES, WIN])
        dt_exp = sb("dt_exp", [P, HALVES, WIN])
        skip = sb("skip", [P, HALVES, WIN])
        decay = sb("decay", [P, RING, HALVES, WIN])
        c_rows = sb("c_rows", [P, RING, WIN])
        h = sb("h", [P, RING, HALVES, WIN])
        hc = sb("hc", [P, 2, HALVES, WIN])
        carry = sb("carry", [P, STATES, HALVES])
        y0 = sb("y0", [P, TOKENS // P, INNER])
        yt = sb("yt", [P, BLOCKS, INNER])
        gated = sb("gated", [P, HALVES, WIN])
        z_in = sb("z_in", [P, HALVES, WIN])
        o = sb("o", [P, BLOCKS, INNER])
        o_t = sb("o_t", [P, HALVES, WIN])
        x_in = sb("x_in", [P, WIN])
        result = sb("result", [P, WIN])
        stats = [sb(f"stats{i}", [P, BLOCKS, 6]) for i in range(2)]
        moments = [sb(f"moments{i}", [P, BLOCKS, 2]) for i in range(2)]
        var_eps = [sb(f"var_eps{i}", [P, BLOCKS]) for i in range(2)]
        rstd = [sb(f"rstd{i}", [P, BLOCKS]) for i in range(2)]
        select_f32 = y0[0:SPREAD, 0:2 * STATES, 0:P]
        dw_all = h[:, :, :, :].rearrange("p a b c -> p (a b c)")[:, 0:TAPS * INNER].rearrange("p (a b) -> p a b", a=TAPS)
        fc1_t = decay[:, 0, 0, 0:INNER]
        edge_scale = decay[0:TAPS + 1, 1, 0, 0:INNER]
        fc2_b_in = c_rows[:, 0, 0:1]

        b_bank = [ps(f"b_bank{i}", [P, WIN]) for i in range(2)]
        u_bank = ps("u_bank", [P, WIN])
        c_bank = ps("c_bank", [P, WIN])
        y_bank = ps("y_bank", [P, BLOCKS, INNER])
        post_bank = ps("post_bank", [P, WIN])
        pre_bank = ps("pre_bank", [P, WIN])

        s_const = sem("constants_loaded")
        s_setup_dve = sem("setup_vector")
        s_setup_act = sem("setup_scalar")
        s_setup_pe = sem("setup_tensor")
        s_halo = sem("halo_loaded")
        s_xi_in = sem("xi_window_loaded")
        s_z_in = sem("z_window_loaded")
        s_x_in = sem("x_window_loaded")
        s_xi_st = sem("xi_stored")
        s_z_st = sem("z_stored")
        s_out_st = sem("output_stored")
        s_b = sem("b_broadcast")
        s_c = sem("c_broadcast")
        s_cc = sem("c_copied")
        s_decay = sem("decay_ready")
        s_u1 = sem("u1_ready")
        s_u0 = sem("u0_ready")
        s_h1 = sem("h1_ready")
        s_h = sem("h_ready")
        s_carry = sem("carry_saved")
        s_hc = sem("hc_ready")
        s_y = sem("y_added")
        s_skip = sem("skip_ready")
        s_skip_y = sem("skip_added")
        s_y0 = sem("y0_saved")
        s_yt = sem("y_total_ready")
        s_low = sem("low_ranks_ready")
        s_high = sem("part_high_ready")
        s_lowdt = sem("low_dt_copied")
        s_rest = sem("part_rest_ready")
        s_mid = sem("part_mid_ready")
        s_parts = sem("parts_ready")
        s_dtp = sem("dt_projected")
        s_lin = sem("dt_linear_copied")
        s_cap = sem("dt_capped")
        s_e = sem("dt_exp_ready")
        s_ln = sem("dt_log_ready")
        s_dt = sem("dt_ready")
        s_dtx = sem("dtx_ready")
        s_conv = sem("conv_ready")
        s_hid = sem("hidden_ready")
        s_xip = sem("xi_projected")
        s_zp = sem("z_projected")
        s_xia = sem("xi_ready")
        s_za = sem("z_ready")
        s_stat = [sem("norm1_stats"), sem("norm2_stats")]
        s_mom = [sem("norm1_moments"), sem("norm2_moments")]
        s_ve = [sem("norm1_var_eps"), sem("norm2_var_eps")]
        s_rstd = [sem("norm1_rstd"), sem("norm2_rstd")]
        s_norm = [sem("norm1_done"), sem("norm2_done")]
        s_t1 = sem("norm1_transposed")
        s_g = sem("norm1_affine_done")
        s_gz = sem("gated_ready")
        s_op = sem("out_projected")
        s_o = sem("out_projection_copied")
        s_t2 = sem("norm2_transposed")
        s_ot = sem("norm2_transposed_copied")
        s_fc2 = sem("fc2_ready")
        s_res = sem("result_ready")

        constants = [
            (ident[:, :], d["ident"]),
            (select_f32, d["select"].rearrange("r (j p) -> r j p", p=P)),
            (part_weight[:, :], d["part_weight"]),
            (dw_all, d["dw_rep"].rearrange("p (t n) -> p t n", t=TAPS)),
            (fc1_t, d["fc1_t"]),
            (edge_w[:, :], d["edge_w"]),
            (edge_scale, d["edge_scale"]),
            (in_w[:, :, :], d["in_w_t"].rearrange("(a p) n -> p a n", p=P)),
            (in_b[:, :], d["in_b"]),
            (A[:, :, :, :], d["A_log"].rearrange("p (k a n) -> p k a n", k=DIRS, a=HALVES)),
            (D[:, :, :], d["Ds"].rearrange("p (k a) -> p k a", k=DIRS)),
            (norm1_w[:, :], d["norm1_w"]),
            (norm1_b[:, :], d["norm1_b"]),
            (norm2_w[:, :], d["norm2_w"]),
            (norm2_b[:, :], d["norm2_b"]),
            (out_w[:, :, :], d["out_w_t"].rearrange("(a p) n -> p a n", p=P)),
            (out_b[:, :], d["out_b"]),
            (fc2_w[:, :, :], d["fc2_w_t"].rearrange("(a p) n -> p a n", p=P)),
            (fc2_b_in, d["fc2_b"]),
        ]
        SETUP_DVE = 9

        block = ctx.enter_context(nc.Block())

        @block.sync
        def _(sp):
            for where, what in constants:
                sp.dma_start(where, what).then_inc(s_const, 16)

            def ahead(*values):
                for v in values:
                    if isinstance(v, bass.AP):
                        sp.lower_ap_dma(v)
                    elif not isinstance(v, int):
                        sp.lower_val(v)

            def load_pre(q, b, hw):
                top, bottom = hw == 0, hw == PRES - 1
                inner = x_halo[:, :, 1:W + 1]
                if top:
                    pieces = [(0, 1, None), (1, ROWS + 2, 0)]
                elif bottom:
                    pieces = [(ROWS + 1, ROWS + 2, None), (0, ROWS + 1, hw * ROWS - 1)]
                else:
                    pieces = [(0, 2, hw * ROWS - 1), (2, ROWS + 2, hw * ROWS + 1)]
                src = [d["zero_row"].rearrange("p (r w) -> p r w", r=1) if row is None
                       else d["x"][b, :, row:row + hi - lo, :] for lo, hi, row in pieces]
                ahead(q, *src)
                wait(sp, s_conv, q)
                if isinstance(q, int) and q == 0:
                    sp.wait_ge(s_setup_dve, SETUP_DVE)
                for (lo, hi, _), rows in zip(pieces, src):
                    sp.dma_start(inner[:, lo:hi, :], rows).then_inc(s_halo, 16)
                sp.dma_start(edge_rows[:, :], d["edge_rows"][hw]).then_inc(s_halo, 16)

            def store_pre(q, b, hw):
                tok = slice(hw * HALF, (hw + 1) * HALF)
                xi_to, z_to = xi_dram[b, :, :, tok], z_dram[b, :, :, tok]
                ahead(q + 1, xi_to, z_to)
                wait(sp, s_xia, q + 1)
                sp.dma_start(xi_to, xi_out[:, :, :]).then_inc(s_xi_st, 16)
                wait(sp, s_za, q + 1)
                sp.dma_start(z_to, z_out[:, :, :]).then_inc(s_z_st, 16)

            def load_window(s1, b, k, win, par, skips=0):
                src = xi_dram[b, :, :, win * WIN:(win + 1) * WIN]
                stored = 16 * (b * PRES + 2 * win + 2)
                ahead(skips, stored, s1 - 1, 2 * s1, src)
                wait(sp, s_skip, skips)
                wait(sp, s_xi_st, stored)
                wait(sp, s_dtx, s1 - 1)
                wait(sp, s_low, s1 - 1)
                wait(sp, s_lin, 2 * s1)
                sp.dma_start(xi[par][:, :, :], src).then_inc(s_xi_in, 16)
                sp.dma_start(low_w[:, :, :], d["low_w"][k].rearrange("(a p) n -> p a n", p=P)).then_inc(s_xi_in, 16)
                sp.dma_start(dt_w[SPREAD:LOW, :], d["dt_w_t"][k]).then_inc(s_xi_in, 16)
                sp.dma_start(dt_b[:, :], d["dt_b"][k]).then_inc(s_xi_in, 16)

            def load_z(p, b, win):
                src = z_dram[b, :, :, win * WIN:(win + 1) * WIN]
                stored = 16 * (b * PRES + 2 * win + 2)
                ahead(p, stored, src)
                wait(sp, s_gz, p)
                wait(sp, s_z_st, stored)
                sp.dma_start(z_in[:, :, :], src).then_inc(s_z_in, 16)

            def load_x(p, b, win):
                src = x_flat[b, :, win * WIN:(win + 1) * WIN]
                ahead(p, src)
                wait(sp, s_res, p)
                sp.dma_start(x_in[:, :], src).then_inc(s_x_in, 16)

            def store_out(p, b, win):
                to = out_flat[b, :, win * WIN:(win + 1) * WIN]
                ahead(p + 1, to)
                wait(sp, s_res, p + 1)
                sp.dma_start(to, result[:, :]).then_inc(s_out_st, 16)

            for hw in range(PRES):
                load_pre(hw, 0, hw)
                store_pre(hw, 0, hw)
            load_window(0, 0, 0, 0, 0)

            def image(b, first, last):
                for i in range(STEPS):
                    k, w = divmod(i, WINS)
                    s = b * STEPS + i
                    q = (b + 1) * PRES + i
                    skips = b * WINS + max(0, i - WINS)
                    if i + 1 < STEPS:
                        k1, w1 = divmod(i + 1, WINS)
                        load_window(s + 1, b, k1, w1 if k1 == 0 else WINS - 1 - w1, (i + 1) % 2, skips)
                    elif not last:
                        load_window(s + 1, b + 1, 0, 0, 0, skips)
                    if k == 1 and w >= 1:
                        load_z(b * WINS + w - 1, b, WINS - w)
                    if k == 1 and w >= 2:
                        load_x(b * WINS + w - 2, b, WINS + 1 - w)
                    if not first and i == 0:
                        load_z(b * WINS - 1, b - 1, 0)
                    if not first and i < 2:
                        load_x(b * WINS - 2 + i, b - 1, 1 - i)
                    if not last:
                        load_pre(q, b + 1, i)
                    if i == 0:
                        if not first:
                            store_pre(q - 1, b, PRES - 1)
                    elif not last:
                        store_pre(q - 1, b + 1, i - 1)
                    if k == 1 and w >= 2:
                        store_out(b * WINS + w - 2, b, WINS + 1 - w)
                    if not first and i < 2:
                        store_out(b * WINS - 2 + i, b - 1, 1 - i)

            image(0, True, False)
            with sp.Fori(1, IMAGES - 1) as b:
                image(b, False, False)
            image(IMAGES - 1, False, True)
            end = IMAGES * WINS
            load_z(end - 1, IMAGES - 1, 0)
            for p in (end - 2, end - 1):
                load_x(p, IMAGES - 1, end - 1 - p)
                store_out(p, IMAGES - 1, end - 1 - p)
            sp.wait_ge(s_xi_st, 16 * IMAGES * PRES)
            sp.wait_ge(s_z_st, 16 * IMAGES * PRES)
            sp.wait_ge(s_out_st, 16 * end)

        @block.tensor
        def _(pe):
            mm = nc.tensor.matmul

            def turn(out, in_, start):
                return mm(out, in_, ident[:, :], is_transpose=True, start=start, stop=True, skip_group_check=True)

            pe.wait_ge(s_const, 16 * len(constants))
            for a in range(HALVES):
                last = mm(post_bank[:, 0:1], fc2_w[:, a, :], norm2_b[:, a:a + 1], start=(a == 0), stop=(a == HALVES - 1))
            last.then_inc(s_setup_pe, 1)

            def conv(q, lo, hi):
                for i in range(lo, hi):
                    a, tap = divmod(i, TAPS + 1)
                    out = pre_bank[:, a * HALF:(a + 1) * HALF]
                    if tap < TAPS:
                        dy, dx = divmod(tap, 3)
                        last = mm(out, conv_w[:, tap, a * P:(a + 1) * P], x_halo[:, dy:dy + ROWS, dx:dx + W],
                                  start=(tap == 0), stop=False)
                    else:
                        last = mm(out, edge_w[:, a * P:(a + 1) * P], edge_rows[:, :], start=False, stop=True)
                if hi == HALVES * (TAPS + 1):
                    last.then_inc(s_conv, 1)

            def in_proj(bank, base, done):
                for a in range(HALVES):
                    out = bank[:, a * HALF:(a + 1) * HALF]
                    cols = slice(base + a * P, base + (a + 1) * P)
                    for c in range(HALVES):
                        mm(out, in_w[:, c, cols], hidden[:, c, :], start=(c == 0), stop=False)
                    last = mm(out, in_b[:, cols], ones[:, :], start=False, stop=True)
                last.then_inc(done, 1)

            def low_ranks(s1, par):
                pe.wait_ge(s_xi_in, 64 * (s1 + 1))
                for c in range(HALVES):
                    last = mm(pre_bank[0:LOW, :], low_w[:, c, :], xi[par][:, c, :], start=(c == 0), stop=(c == HALVES - 1))
                last.then_inc(s_low, 1)

            def dt_proj(s1, a):
                if a == 0:
                    pe.wait_ge(s_lowdt, s1 + 1)
                    pe.wait_ge(s_rest, s1 + 1)
                else:
                    pe.wait_ge(s_lin, 2 * s1 + 1)
                mm(pre_bank[:, :], dt_w[SPREAD:LOW, a * P:(a + 1) * P], low_dt[SPREAD:LOW, :],
                   start=True, stop=True).then_inc(s_dtp, 1)

            def add_y(s, n, left, st):
                pe.wait_ge(s_hc, s * STATES + n + 1)
                if n == 0:
                    if left == 0:
                        pe.wait_ge(s_y0, st.kept_before + 1)
                    elif left == 1:
                        pe.wait_ge(s_yt, st.p1 + 1)
                for a in range(HALVES):
                    for j in range(BLOCKS):
                        last = turn(y_bank[:, j, a * P:(a + 1) * P], hc[:, n % 2, a, j * P:(j + 1) * P],
                                    start=(n == 0 and a == 0 and j % 2 == 0))
                last.then_inc(s_y, 1)

            def add_skip(count):
                pe.wait_ge(s_skip, count)
                for a in range(HALVES):
                    for j in range(BLOCKS):
                        last = turn(y_bank[:, j, a * P:(a + 1) * P], skip[:, a, j * P:(j + 1) * P], start=False)
                last.then_inc(s_skip_y, 1)

            def turn1(p, a):
                if a == 0:
                    pe.wait_ge(s_norm[0], p + 1)
                else:
                    pe.wait_ge(s_g, 2 * p + 1)
                for j in range(BLOCKS):
                    last = turn(post_bank[:, j * P:(j + 1) * P], yt[:, j, a * P:(a + 1) * P], start=True)
                last.then_inc(s_t1, 1)

            def out_proj(p, a):
                if a == 0:
                    pe.wait_ge(s_gz, p + 1)
                else:
                    pe.wait_ge(s_o, 2 * p + 1)
                for jj in range(2):
                    j = 2 * a + jj
                    out = post_bank[:, jj * INNER:(jj + 1) * INNER]
                    for c in range(HALVES):
                        mm(out, gated[:, c, j * P:(j + 1) * P], out_w[:, c, :], start=(c == 0), stop=False)
                    last = mm(out, ones[:, 0:P], out_b[:, :], start=False, stop=True)
                last.then_inc(s_op, 1)

            def turn2(p, a):
                if a == 0:
                    pe.wait_ge(s_norm[1], p + 1)
                else:
                    pe.wait_ge(s_ot, 2 * p + 1)
                for j in range(BLOCKS):
                    last = turn(post_bank[:, j * P:(j + 1) * P], o[:, j, a * P:(a + 1) * P], start=True)
                last.then_inc(s_t2, 1)

            def fc2(p):
                pe.wait_ge(s_ot, 2 * p + 2)
                for c in range(HALVES):
                    last = mm(post_bank[:, :], fc2_w[:, c, :], o_t[:, c, :], start=(c == 0), stop=(c == HALVES - 1))
                last.then_inc(s_fc2, 1)

            pe.wait_ge(s_setup_dve, SETUP_DVE)
            pe.wait_ge(s_setup_act, 2)
            def pre_alone(q):
                pe.wait_ge(s_halo, 48 * (q + 1))
                wait(pe, s_xia, q)
                conv(q, 0, HALVES * (TAPS + 1))
                pe.wait_ge(s_hid, q + 1)
                in_proj(pre_bank, 0, s_xip)
                wait(pe, s_za, q)
                in_proj(post_bank, INNER, s_zp)

            pre_alone(0)
            with pe.Fori(1, PRES) as q:
                pre_alone(q)
            pe.wait_ge(s_xia, PRES)
            pe.wait_ge(s_za, PRES)
            low_ranks(0, 0)
            dt_proj(0, 0)
            dt_proj(0, 1)

            def step(st):
                s, par, nxt = st.s, st.parity, 1 - st.parity
                for n in range(STATES):
                    if n == 0:
                        pe.wait_ge(s_parts, s + 1)
                    wait(pe, s_h, s * STATES + n - 1)
                    mm(b_bank[n % 2][:, :], select[:, n, :], parts[par][:, :], start=True, stop=True).then_inc(s_b, 1)
                    wait(pe, s_cc, s * STATES + n)
                    mm(c_bank[:, :], select[:, STATES + n, :], parts[par][:, :], start=True, stop=True).then_inc(s_c, 1)
                    if n >= LAG:
                        add_y(s, n - LAG, st.left, st)
                    elif not st.first:
                        add_y(s - 1, STATES - LAG + n, None, st)
                    if st.k == 1 and n == 8:
                        add_skip(st.b * WINS + st.w + 1)
                    if not st.last:
                        if n == 3:
                            if st.finish:
                                pe.wait_ge(s_xia, st.pre_index)
                            low_ranks(s + 1, nxt)
                        if n == 6:
                            dt_proj(s + 1, 0)
                        if n == 7:
                            dt_proj(s + 1, 1)
                    if st.pre:
                        if n == 9:
                            pe.wait_ge(s_halo, 48 * (st.pre_index + 1))
                            pe.wait_ge(s_lin, 2 * (s + 1) + 2)
                        if 9 <= n < 13:
                            conv(st.pre_index, 5 * (n - 9), 5 * (n - 8))
                        if n == 14:
                            pe.wait_ge(s_hid, st.pre_index + 1)
                            in_proj(pre_bank, 0, s_xip)
                    if n == 1 and st.finish:
                        if st.post1_before:
                            pe.wait_ge(s_o, 2 * st.p1_before + 2)
                        in_proj(post_bank, INNER, s_zp)
                    if st.post2:
                        if n == 4:
                            if st.finish:
                                pe.wait_ge(s_za, st.pre_index)
                            turn2(st.p2, 0)
                        if n == 6:
                            turn2(st.p2, 1)
                        if n == 8:
                            fc2(st.p2)
                    if st.post1:
                        if n == 10:
                            if st.post2:
                                pe.wait_ge(s_res, st.p2 + 1)
                            elif st.finish:
                                pe.wait_ge(s_za, st.pre_index)
                            turn1(st.p1, 0)
                        if n == 12:
                            turn1(st.p1, 1)
                        if n == 14:
                            out_proj(st.p1, 0)
                        if n == 15:
                            out_proj(st.p1, 1)

            walk(pe, step)
            end = IMAGES * WINS
            s_end = IMAGES * STEPS
            for n in range(STATES - LAG, STATES):
                add_y(s_end - 1, n, None, None)
            for p in (end - 2, end - 1):
                if p == end - 1:
                    pe.wait_ge(s_res, p)
                    turn1(p, 0)
                    turn1(p, 1)
                    out_proj(p, 0)
                    out_proj(p, 1)
                turn2(p, 0)
                turn2(p, 1)
                fc2(p)

        @block.scalar
        def _(act):
            run = nc.scalar.activation
            nc.scalar.preload_act_table_set(LN_EXP_SET)
            act.wait_ge(s_const, 16 * len(constants))
            run(A[:, :, :, :], A[:, :, :, :], ACT.Exp).then_inc(s_setup_act, 1)
            nc.scalar.copy(select[:, :, :], select_f32).then_inc(s_setup_act, 1)

            def silu_hidden(q):
                act.wait_ge(s_conv, q + 1)
                run(hidden[:, :, :], pre_bank[:, :].rearrange("p (a n) -> p a n", a=HALVES), ACT.Silu).then_inc(s_hid, 1)

            def silu_xi_z(q):
                act.wait_ge(s_xip, q + 1)
                wait(act, s_xi_st, 16 * q)
                run(xi_out[:, :, :], pre_bank[:, :].rearrange("p (a n) -> p a n", a=HALVES), ACT.Silu).then_inc(s_xia, 1)
                act.wait_ge(s_zp, q + 1)
                wait(act, s_z_st, 16 * q)
                run(z_out[:, :, :], post_bank[:, :].rearrange("p (a n) -> p a n", a=HALVES), ACT.Silu).then_inc(s_za, 1)

            def split_high(s1):
                act.wait_ge(s_low, s1 + 1)
                nc.scalar.copy(part_high[:, :], pre_bank[0:SPREAD, :]).then_inc(s_high, 1)
                nc.scalar.copy(low_dt[SPREAD:LOW, :], pre_bank[SPREAD:LOW, :]).then_inc(s_lowdt, 1)

            def split_mid(s1):
                act.wait_ge(s_rest, s1 + 1)
                wait(act, s_parts, s1)
                nc.scalar.copy(part_mid[:, :], part_rest[:, :]).then_inc(s_mid, 1)

            def dt_linear(s1, a):
                act.wait_ge(s_dtp, 2 * s1 + a + 1)
                if a == 0:
                    wait(act, s_dt, s1)
                run(dt_lin[:, a, :], pre_bank[:, :], ACT.Identity, bias=dt_b[:, a:a + 1]).then_inc(s_lin, 1)

            def dt_softplus(s1):
                act.wait_ge(s_cap, s1 + 1)
                run(dt_exp[:, :, :], dt_exp[:, :, :], ACT.Exp).then_inc(s_e, 1)
                act.wait_ge(s_e, s1 + 1)
                run(dt_exp[:, :, :], dt_exp[:, :, :], ACT.Ln, bias=1.0).then_inc(s_ln, 1)

            def decays(st, n):
                s = st.s
                if n == 0:
                    act.wait_ge(s_dt, s + 1)
                wait(act, s_h, s * STATES + n - RING + 1)
                for a in range(HALVES):
                    last = run(decay[:, n % RING, a, :], dt[st.parity][:, a, :], ACT.Exp, scale=A[:, st.k, a, n:n + 1])
                last.then_inc(s_decay, 1)

            def affine1(p, a):
                act.wait_ge(s_t1, 2 * p + a + 1)
                run(gated[:, a, :], post_bank[:, :], ACT.Identity, bias=norm1_b[:, a:a + 1],
                    scale=norm1_w[:, a:a + 1]).then_inc(s_g, 1)

            def copy_o(p, a):
                act.wait_ge(s_op, 2 * p + a + 1)
                nc.scalar.copy(o[:, 2 * a:2 * a + 2, :], post_bank[:, :].rearrange("p (j n) -> p j n", j=2)).then_inc(s_o, 1)

            def copy_ot(p, a):
                act.wait_ge(s_t2, 2 * p + a + 1)
                if a == 0:
                    wait(act, s_fc2, p)
                nc.scalar.copy(o_t[:, a, :], post_bank[:, :]).then_inc(s_ot, 1)

            nc.scalar.preload_act_table_set(SILU_SET)
            silu_hidden(0)
            silu_xi_z(0)
            with act.Fori(1, PRES) as q:
                silu_hidden(q)
                silu_xi_z(q)
            nc.scalar.preload_act_table_set(LN_EXP_SET)
            act.wait_ge(s_setup_dve, SETUP_DVE)
            split_high(0)
            split_mid(0)
            dt_linear(0, 0)
            dt_linear(0, 1)
            dt_softplus(0)

            def step(st):
                s, par = st.s, st.parity
                decays(st, 0)
                decays(st, 1)
                for n in range(STATES):
                    act.wait_ge(s_c, s * STATES + n + 1)
                    wait(act, s_hc, s * STATES + n - RING + 1)
                    nc.scalar.copy(c_rows[:, n % RING, :], c_bank[:, :]).then_inc(s_cc, 1)
                    if n + 2 < STATES:
                        decays(st, n + 2)
                    if n == 0:
                        if st.post1_before:
                            copy_o(st.p1_before, 1)
                        if st.k == 1:
                            wait(act, s_skip_y, st.b * WINS + st.w)
                            act.wait_ge(s_xi_in, 64 * (s + 1))
                            for a in range(HALVES):
                                last = run(skip[:, a, :], xi[par][:, a, :], ACT.Copy, scale=D_sum[:, a:a + 1])
                            last.then_inc(s_skip, 1)
                    if n == 2:
                        if st.keep_y0:
                            act.wait_ge(s_y, s * STATES)
                            wait(act, s_yt, st.b * WINS)
                            nc.scalar.copy(y0[:, blocks_of(st.keep_window), :], y_bank[:, :, :]).then_inc(s_y0, 1)
                        if st.finish:
                            nc.scalar.preload_act_table_set(SILU_SET)
                            silu_xi_z(st.pre_index - 1)
                            nc.scalar.preload_act_table_set(LN_EXP_SET)
                    if not st.last:
                        if n == 4:
                            split_high(s + 1)
                        if n == 5:
                            split_mid(s + 1)
                        if n == 7:
                            dt_linear(s + 1, 0)
                        if n == 8:
                            dt_linear(s + 1, 1)
                        if n == 10:
                            dt_softplus(s + 1)
                    if st.pre and n == 13:
                        nc.scalar.preload_act_table_set(SILU_SET)
                        silu_hidden(st.pre_index)
                        nc.scalar.preload_act_table_set(LN_EXP_SET)
                    if st.post2:
                        if n == 5:
                            copy_ot(st.p2, 0)
                        if n == 7:
                            copy_ot(st.p2, 1)
                    if st.post1:
                        if n == 11:
                            affine1(st.p1, 0)
                        if n == 13:
                            affine1(st.p1, 1)
                        if n == 15:
                            copy_o(st.p1, 0)

            walk(act, step)
            end = IMAGES * WINS
            copy_o(end - 2, 1)
            for p in (end - 2, end - 1):
                if p == end - 1:
                    affine1(p, 0)
                    affine1(p, 1)
                    copy_o(p, 0)
                    copy_o(p, 1)
                copy_ot(p, 0)
                copy_ot(p, 1)

        @block.vector
        def _(dve):
            V = nc.vector
            dve.wait_ge(s_const, 16 * len(constants))
            V.memset(x_halo[:, :, :], 0.0).then_inc(s_setup_dve, 1)
            V.memset(ones[:, :], 1.0).then_inc(s_setup_dve, 1)
            V.memset(minus_half[:, :], -0.5).then_inc(s_setup_dve, 1)
            V.tensor_tensor(conv_w[:, :, :], dw_all, fc1_t.rearrange("p (t n) -> p t n", t=1).broadcast_to((P, TAPS, INNER)),
                            ALU.mult).then_inc(s_setup_dve, 1)
            V.tensor_tensor(edge_w[:, :], edge_w[:, :], edge_scale, ALU.mult).then_inc(s_setup_dve, 1)
            V.tensor_tensor(D_sum[:, :], D[:, 0, :], D[:, 1, :], ALU.add).then_inc(s_setup_dve, 1)
            dve.wait_ge(s_setup_act, 1)
            V.tensor_scalar(A[:, :, :, :], A[:, :, :, :], -1.0, None, ALU.mult).then_inc(s_setup_dve, 1)
            dve.wait_ge(s_setup_pe, 1)
            V.tensor_tensor(fc2_b[:, :], post_bank[:, 0:1], fc2_b_in, ALU.add).then_inc(s_setup_dve, 1)
            V.tensor_tensor(fc2_w[:, :, :], fc2_w[:, :, :],
                            norm2_w[:, :].rearrange("p (a n) -> p a n", n=1).broadcast_to((P, HALVES, DIM)),
                            ALU.mult).then_inc(s_setup_dve, 1)
            dve.wait_ge(s_setup_dve, SETUP_DVE)

            def split_rest(s1):
                dve.wait_ge(s_high, s1 + 1)
                V.scalar_tensor_tensor(out=part_rest[:, :], in0=part_high[:, :], scalar=part_weight[:, 0:1],
                                       in1=pre_bank[0:SPREAD, :], op0=ALU.mult, op1=ALU.add).then_inc(s_rest, 1)

            def split_low(s1, par):
                dve.wait_ge(s_mid, s1 + 1)
                V.scalar_tensor_tensor(out=parts[par][:, :], in0=part_mid[:, :], scalar=part_weight[:, 1:2],
                                       in1=part_rest[:, :], op0=ALU.mult, op1=ALU.add).then_inc(s_parts, 1)

            def dt_cap(s1):
                dve.wait_ge(s_lin, 2 * s1 + 2)
                V.tensor_scalar(dt_exp[:, :, :], dt_lin[:, :, :], EXP_CAP, None, ALU.min).then_inc(s_cap, 1)

            def dt_max(s1, par):
                dve.wait_ge(s_ln, s1 + 1)
                V.tensor_tensor(dt[par][:, :, :], dt_exp[:, :, :], dt_lin[:, :, :], ALU.max).then_inc(s_dt, 1)

            def dt_times_x(s1, par):
                dve.wait_ge(s_xi_in, 64 * (s1 + 1))
                dve.wait_ge(s_dt, s1 + 1)
                V.tensor_tensor(dtx[par][:, :, :], dt[par][:, :, :], xi[par][:, :, :], ALU.mult).then_inc(s_dtx, 1)

            def norm_stats(i, src, p):
                for j in range(BLOCKS):
                    V.bn_stats(stats[i][:, j, :], src[:, j, :]).then_inc(s_stat[i], 1)
                dve.wait_ge(s_stat[i], BLOCKS * (p + 1))
                V.memset(var_eps[i][:, :], EPS).then_inc(s_ve[i], 1)
                for j in range(BLOCKS):
                    V.bn_aggr(moments[i][:, j, :], stats[i][:, j, :]).then_inc(s_mom[i], 1)
                dve.wait_ge(s_ve[i], 2 * p + 1)
                dve.wait_ge(s_mom[i], BLOCKS * (p + 1))
                V.tensor_tensor(var_eps[i][:, :], var_eps[i][:, :], moments[i][:, :, 1], ALU.add).then_inc(s_ve[i], 1)

            def normalize(i, src, p):
                dve.wait_ge(s_rstd[i], p + 1)
                for j in range(BLOCKS):
                    last = V.tensor_scalar(src[:, j, :], src[:, j, :], moments[i][:, j, 0:1], rstd[i][:, j:j + 1],
                                           ALU.subtract, ALU.mult)
                last.then_inc(s_norm[i], 1)

            def total_y(s, p, window):
                dve.wait_ge(s_y, s * STATES)
                dve.wait_ge(s_skip_y, p + 1)
                wait(dve, s_t1, 2 * p)
                dve.wait_ge(s_y0, p + 1)
                V.tensor_tensor(yt[:, :, :], y_bank[:, :, :], y0[:, blocks_of(window), :],
                                ALU.add).then_inc(s_yt, 1)
                dve.wait_ge(s_yt, p + 1)

            def finish_out(p):
                dve.wait_ge(s_fc2, p + 1)
                dve.wait_ge(s_x_in, 16 * (p + 1))
                wait(dve, s_out_st, 16 * p)
                V.scalar_tensor_tensor(out=result[:, :], in0=post_bank[:, :], scalar=fc2_b[:, 0:1], in1=x_in[:, :],
                                       op0=ALU.add, op1=ALU.add).then_inc(s_res, 1)

            split_rest(0)
            split_low(0, 0)
            dt_cap(0)
            dt_max(0, 0)
            dt_times_x(0, 0)

            def step(st):
                s, par, nxt, k = st.s, st.parity, 1 - st.parity, st.k
                way = slice(None) if k == 0 else slice(WIN - 1, None, -1)
                end = WIN - 1 if k == 0 else 0
                for n in range(STATES):
                    count = s * STATES + n
                    if n == 0:
                        dve.wait_ge(s_dtx, s + 1)
                    dve.wait_ge(s_b, count + 1)
                    wait(dve, s_h1, count)
                    V.tensor_tensor(u_bank[:, :], dtx[par][:, 1, :], b_bank[n % 2][:, :], ALU.mult).then_inc(s_u1, 1)
                    dve.wait_ge(s_u1, count + 1)
                    V.tensor_tensor(b_bank[n % 2][:, :], dtx[par][:, 0, :], b_bank[n % 2][:, :], ALU.mult).then_inc(s_u0, 1)
                    dve.wait_ge(s_decay, count + 1)
                    wait(dve, s_hc, count - RING + 1)
                    zero = st.static_w == 0
                    if not zero:
                        dve.wait_ge(s_carry, (s - 1) * (STATES // RING) + n // RING + 1)
                    V.tensor_tensor_scan(h[:, n % RING, 1, way], decay[:, n % RING, 1, way], u_bank[:, way],
                                         0.0 if zero else carry[:, n, 1:2], ALU.mult, ALU.add).then_inc(s_h1, 1)
                    dve.wait_ge(s_u0, count + 1)
                    V.tensor_tensor_scan(h[:, n % RING, 0, way], decay[:, n % RING, 0, way], b_bank[n % 2][:, way],
                                         0.0 if zero else carry[:, n, 0:1], ALU.mult, ALU.add).then_inc(s_h, 1)
                    if n % RING == RING - 1:
                        dve.wait_ge(s_h, count + 1)
                        V.tensor_copy(carry[:, n - RING + 1:n + 1, :], h[:, :, :, end]).then_inc(s_carry, 1)
                    if not st.last:
                        if n == 4:
                            split_rest(s + 1)
                        if n == 5:
                            split_low(s + 1, nxt)
                        if n == 9:
                            dt_cap(s + 1)
                        if n == 11:
                            dt_max(s + 1, nxt)
                        if n == 12:
                            dt_times_x(s + 1, nxt)
                    if st.post2:
                        if n == 1:
                            dve.wait_ge(s_o, 2 * st.p2 + 2)
                            norm_stats(1, o, st.p2)
                        if n == 3:
                            normalize(1, o, st.p2)
                        if n == 8:
                            finish_out(st.p2)
                    if st.post1:
                        if n == 2:
                            total_y(s, st.p1, st.p1_window)
                            norm_stats(0, yt, st.p1)
                        if n == 5:
                            normalize(0, yt, st.p1)

            walk(dve, step)
            end = IMAGES * WINS
            total_y(IMAGES * STEPS, end - 1, 0)
            norm_stats(0, yt, end - 1)
            normalize(0, yt, end - 1)
            for p in (end - 2, end - 1):
                dve.wait_ge(s_o, 2 * p + 2)
                norm_stats(1, o, p)
                normalize(1, o, p)
                finish_out(p)

        @block.gpsimd
        def _(pool):
            G = nc.gpsimd

            def inverse_root(i, p):
                pool.wait_ge(s_ve[i], 2 * p + 2)
                G.tensor_tensor(rstd[i][:, :], var_eps[i][:, :], minus_half[:, :], ALU.pow).then_inc(s_rstd[i], 1)

            def gate(p):
                pool.wait_ge(s_g, 2 * p + 2)
                pool.wait_ge(s_z_in, 16 * (p + 1))
                G.tensor_tensor(gated[:, :, :], gated[:, :, :], z_in[:, :, :], ALU.mult).then_inc(s_gz, 1)

            pool.wait_ge(s_setup_dve, SETUP_DVE)

            def step(st):
                for n in range(STATES):
                    count = st.s * STATES + n
                    pool.wait_ge(s_h, count + 1)
                    pool.wait_ge(s_cc, count + 1)
                    wait(pool, s_y, count - 1)
                    G.tensor_tensor(hc[:, n % 2, :, :], h[:, n % RING, :, :],
                                    c_rows[:, n % RING, :].rearrange("p (a n) -> p a n", a=1).broadcast_to((P, HALVES, WIN)),
                                    ALU.mult).then_inc(s_hc, 1)
                    if st.post2 and n == 1:
                        inverse_root(1, st.p2)
                    if st.post1 and n == 3:
                        inverse_root(0, st.p1)
                    if st.post1 and n == 13:
                        gate(st.p1)

            walk(pool, step)
            end = IMAGES * WINS
            inverse_root(0, end - 1)
            inverse_root(1, end - 2)
            gate(end - 1)
            inverse_root(1, end - 1)


def edge_table():
    inside = np.ones((PRES, TAPS + 1, ROWS, W), np.float32)
    for tap in range(TAPS):
        dy, dx = divmod(tap, 3)
        if dy == 0:
            inside[0, tap, 0, :] = 0
        if dy == 2:
            inside[PRES - 1, tap, ROWS - 1, :] = 0
        if dx == 0:
            inside[:, tap, :, 0] = 0
        if dx == 2:
            inside[:, tap, :, W - 1] = 0
    return inside.reshape(PRES, TAPS + 1, HALF)


def select_table():
    table = np.zeros((SPREAD, 2 * STATES, P), np.float32)
    for r in range(SPREAD):
        table[r, r % (2 * STATES), :] = 1
    return table.reshape(SPREAD, 2 * STATES * P)


def part_table():
    table = np.zeros((SPREAD, 2), np.float32)
    table[2 * STATES:, 0] = -1
    table[4 * STATES:, 1] = -1
    return table


def kernel(**inputs):
    import concourse.bacc as bacc
    from concourse.bass_utils import run_bass_kernel_spmd

    get = {n.removeprefix("L0_conv_"): np.asarray(a) for n, a in inputs.items()}
    xw = get["x_proj_w"]
    bc = xw[:, RANK:, :]
    one_row = np.ones((1, INNER), np.float32)
    arrays = {
        "x": get["x"],
        "ident": np.eye(P, dtype=np.float32),
        "select": select_table(),
        "part_weight": part_table(),
        "edge_rows": edge_table(),
        "zero_row": np.zeros((P, W), np.float32),
        "fc1_t": get["fc1_w"].T,
        "dw_rep": np.broadcast_to(get["dw_w"].reshape(INNER, TAPS).T.reshape(1, TAPS * INNER), (P, TAPS * INNER)),
        "edge_w": np.concatenate([get["dw_w"].reshape(INNER, TAPS).T, get["dw_b"].reshape(1, INNER)]),
        "edge_scale": np.concatenate([np.broadcast_to(get["fc1_b"].reshape(1, INNER), (TAPS, INNER)), one_row]),
        "in_w_t": get["in_proj_w"].T,
        "in_b": get["in_proj_b"].reshape(1, 2 * INNER),
        "low_w": np.concatenate([bc, bc, bc, xw[:, :RANK, :]], axis=1).transpose(0, 2, 1),
        "dt_w_t": get["dt_proj_w"].transpose(0, 2, 1),
        "dt_b": get["dt_proj_b"].reshape(DIRS, HALVES, P).transpose(0, 2, 1),
        "A_log": get["A_log"].reshape(DIRS, HALVES, P, STATES).transpose(2, 0, 1, 3).reshape(P, -1),
        "Ds": get["Ds"].reshape(DIRS, HALVES, P).transpose(2, 0, 1).reshape(P, -1),
        "norm1_w": get["out_norm_w"].reshape(HALVES, P).T,
        "norm1_b": get["out_norm_b"].reshape(HALVES, P).T,
        "norm2_w": get["norm_w"].reshape(HALVES, P).T,
        "norm2_b": get["norm_b"].reshape(HALVES, P).T,
        "out_w_t": get["out_proj_w"].T,
        "out_b": get["out_proj_b"].reshape(1, INNER),
        "fc2_w_t": get["fc2_w"].T,
        "fc2_b": get["fc2_b"].reshape(DIM, 1),
    }
    nc = bacc.Bacc("TRN2", target_bir_lowering=False, num_devices=1)
    feed, d = {}, {}
    for name, a in arrays.items():
        a = np.ascontiguousarray(a)
        feed[f"in_{name}"] = a
        d[name] = nc.dram_tensor(f"in_{name}", a.shape, mybir.dt.from_np(a.dtype), kind="ExternalInput").ap()
    d["out"] = nc.dram_tensor("out_0", (IMAGES, DIM, H, W), F32, kind="ExternalOutput").ap()
    build(nc, d)
    r = run_bass_kernel_spmd(nc, [feed], core_ids=[0])
    return r.results[0]["out_0"]
```

```python
from contextlib import ExitStack

import numpy as np

import concourse.bass as bass
from concourse import mybir

ALU = mybir.AluOpType
ACT = mybir.ActivationFunctionType
F32 = mybir.dt.float32
BF16 = mybir.dt.bfloat16

IMAGES, DIM, H, W = 16, 128, 64, 64
P = 128
INNER, STATES, RANK, DIRS = 256, 16, 16, 2
HALVES = INNER // P
TOKENS = H * W
WIN = 512
WINS = TOKENS // WIN
BLOCKS = WIN // P
HALF = WIN // 2
PRES = TOKENS // HALF
ROWS = HALF // W
STEPS = DIRS * WINS
TAPS = 9
PARTS = 3
SPREAD = PARTS * STATES
C_AT, DT_AT = 64, 96
LOW = DT_AT + RANK
EPS = 1e-6
RING = 4
LAG = 3
CONV_SLOTS = range(7, 13)
CONV_CUTS = (0, 4, 8, 11, 14, 17, 20)
C_PAIRS = 4
C_RING = 2 * C_PAIRS
LN_EXP_SET = "natural_log_exp_and_others"
SILU_SET = "silu_and_others"


class Step:

    def __init__(self, b, k, w, parity, first_image, last_image):
        self.b, self.k, self.w, self.parity = b, k, w, parity
        self.s = b * STEPS + k * WINS + w
        self.static_w = w if isinstance(w, int) else None
        w0 = self.static_w
        self.first = first_image and k == 0 and w0 == 0
        self.last = last_image and k == 1 and w0 == WINS - 1
        self.pre = not last_image
        self.pre_index = (b + 1) * PRES + k * WINS + w
        if self.first:
            self.finish = False
        elif last_image:
            self.finish = k == 0 and w0 == 0
        else:
            self.finish = True
        if w0 == 0:
            self.left = None if self.first else (1 - k)
        else:
            self.left = k
        self.keep_y0 = self.left == 0
        self.keep_window = WINS - 1 if (k == 1 and w0 == 0) else w - 1
        self.kept_before = b * WINS + self.keep_window
        if k == 1:
            self.post1 = w0 is None or w0 >= 1
            self.post2 = w0 is None or w0 >= 2
            self.p1 = b * WINS + w - 1
            self.p2 = b * WINS + w - 2
            self.p1_window, self.p2_window = w * -1 + WINS, w * -1 + (WINS + 1)
        else:
            self.post1 = w0 == 0 and not first_image
            self.post2 = w0 in (0, 1) and not first_image
            self.p1 = b * WINS - 1
            self.p1_window = 0
            self.p2 = b * WINS - 2 + w
            self.p2_window = 1 - w if w0 in (0, 1) else 0


def walk(engine, do_step):

    def image(b, first, last):
        for k in range(DIRS):
            head = WINS if first and k == 1 else 2
            for w in range(head):
                do_step(Step(b, k, w, w % 2, first, last))
            if head < WINS:
                with engine.Fori(1, WINS // 2 - 1) as j:
                    for par in range(2):
                        do_step(Step(b, k, 2 * j + par, par, first, last))
                for w in range(WINS - 2, WINS):
                    do_step(Step(b, k, w, w % 2, first, last))

    image(0, True, False)
    with engine.Fori(1, IMAGES - 1) as b:
        image(b, False, False)
    image(IMAGES - 1, False, True)


def blocks_of(window):
    if isinstance(window, int):
        return slice(window * BLOCKS, (window + 1) * BLOCKS)
    return bass.ds(window * BLOCKS, BLOCKS)


def wait(engine, sem, value):
    if isinstance(value, int) and value <= 0:
        return
    engine.wait_ge(sem, value)


def build(nc, d):
    ctx = ExitStack()
    with ctx:
        def sb(name, shape, dt=F32):
            return ctx.enter_context(nc.sbuf_tensor(name, shape, dt))

        def ps(name, shape):
            return ctx.enter_context(nc.psum_tensor(name, shape, F32))

        def sem(name):
            return ctx.enter_context(nc.semaphore(name))

        x_flat = d["x"].rearrange("b c h w -> b c (h w)")
        out_flat = d["out"].rearrange("b c h w -> b c (h w)")
        c_dram = nc.dram_tensor("c_scratch", (2, STATES, WIN), F32, kind="Internal").ap()
        xi_dram = nc.dram_tensor("xi_scratch", (IMAGES, P, HALVES, TOKENS), F32, kind="Internal").ap()
        z_dram = nc.dram_tensor("z_scratch", (IMAGES, P, HALVES, TOKENS), F32, kind="Internal").ap()

        ident = sb("ident", [P, P])
        select = sb("select", [SPREAD, STATES, P], BF16)
        minus = sb("minus", [SPREAD, 2, LOW], BF16)
        conv_w = sb("conv_w", [P, TAPS, INNER])
        edge_w = sb("edge_w", [TAPS + 1, INNER])
        in_w = sb("in_w", [P, HALVES, 2 * INNER])
        in_b = sb("in_b", [1, 2 * INNER])
        ones = sb("ones", [1, HALF])
        low_w = sb("low_w", [P, HALVES, LOW])
        dt_w = sb("dt_w", [LOW, INNER])
        dt_b = sb("dt_b", [P, HALVES])
        A = sb("A", [P, DIRS, HALVES, STATES])
        D = sb("D", [P, DIRS, HALVES])
        D_sum = sb("D_sum", [P, HALVES])
        norm1_w = sb("norm1_w", [P, HALVES])
        norm1_b = sb("norm1_b", [P, HALVES])
        norm2_w = sb("norm2_w", [P, HALVES])
        norm2_b = sb("norm2_b", [P, HALVES])
        out_w = sb("out_w", [P, HALVES, INNER])
        out_b = sb("out_b", [1, INNER])
        fc2_w = sb("fc2_w", [P, HALVES, DIM])
        fc2_b = sb("fc2_b", [P, 1])
        minus_half = sb("minus_half", [P, BLOCKS])

        x_halo = sb("x_halo", [P, ROWS + 2, W + 2])
        edge_rows = sb("edge_rows", [TAPS + 1, HALF])
        hidden = sb("hidden", [P, HALVES, HALF])
        xi_out = sb("xi_out", [P, HALVES, HALF])
        z_out = sb("z_out", [P, HALVES, HALF])
        xi = [sb(f"xi{i}", [P, HALVES, WIN]) for i in range(2)]
        dt = [sb(f"dt{i}", [P, HALVES, WIN]) for i in range(2)]
        dtx = [sb(f"dtx{i}", [P, HALVES, WIN]) for i in range(2)]
        parts = [sb(f"parts{i}", [SPREAD, WIN], BF16) for i in range(2)]
        part_high = sb("part_high", [SPREAD, WIN], BF16)
        part_mid = sb("part_mid", [SPREAD, WIN], BF16)
        low_rows = sb("low_rows", [LOW, WIN])
        dt_lin = sb("dt_lin", [P, HALVES, WIN])
        dt_exp = sb("dt_exp", [P, HALVES, WIN])
        skip = sb("skip", [P, HALVES, WIN])
        decay = sb("decay", [P, RING, HALVES, WIN])
        c_rows = sb("c_rows", [P, C_RING, WIN])
        h = sb("h", [P, RING, HALVES, WIN])
        hc = sb("hc", [P, RING, HALVES, WIN])
        carry = sb("carry", [P, STATES, HALVES])
        y0 = sb("y0", [P, TOKENS // P, INNER])
        yt = sb("yt", [P, BLOCKS, INNER])
        gated = sb("gated", [P, HALVES, WIN])
        z_in = sb("z_in", [P, HALVES, WIN])
        o = sb("o", [P, BLOCKS, INNER])
        o_t = sb("o_t", [P, HALVES, WIN])
        x_in = sb("x_in", [P, WIN])
        result = sb("result", [P, WIN])
        stats = [sb(f"stats{i}", [P, BLOCKS, 6]) for i in range(2)]
        moments = [sb(f"moments{i}", [P, BLOCKS, 2]) for i in range(2)]
        shift = [sb(f"shift{i}", [P, BLOCKS]) for i in range(2)]
        var_eps = [sb(f"var_eps{i}", [P, BLOCKS]) for i in range(2)]
        rstd = [sb(f"rstd{i}", [P, BLOCKS]) for i in range(2)]
        select_f32 = y0[0:SPREAD, 0:STATES, 0:P]
        minus_f32 = y0[0:SPREAD, STATES:STATES + 2, 0:LOW]
        dw_all = h[:, :, :, :].rearrange("p a b c -> p (a b c)")[:, 0:TAPS * INNER].rearrange("p (a b) -> p a b", a=TAPS)
        fc1_t = decay[:, 0, 0, 0:INNER]
        edge_scale = decay[0:TAPS + 1, 1, 0, 0:INNER]
        fc2_b_in = c_rows[:, 0, 0:1]

        b_bank = [ps(f"b_bank{i}", [P, WIN]) for i in range(2)]
        u_bank = [ps(f"u_bank{a}", [P, WIN]) for a in range(HALVES)]
        y_bank = ps("y_bank", [P, BLOCKS, INNER])
        post_bank = ps("post_bank", [P, WIN])
        pre_bank = ps("pre_bank", [P, WIN])

        s_const = sem("constants_loaded")
        s_setup_dve = sem("setup_vector")
        s_setup_act = sem("setup_scalar")
        s_setup_pe = sem("setup_tensor")
        s_halo = sem("halo_loaded")
        s_xi_in = sem("xi_window_loaded")
        s_z_in = sem("z_window_loaded")
        s_x_in = sem("x_window_loaded")
        s_xi_st = sem("xi_stored")
        s_z_st = sem("z_stored")
        s_out_st = sem("output_stored")
        s_b = sem("b_broadcast")
        s_cst = sem("c_stored")
        s_c = [sem(f"c_pair{i}_loaded") for i in range(C_PAIRS)]
        s_decay = sem("decay_ready")
        s_u1 = sem("u1_ready")
        s_u0 = sem("u0_ready")
        s_h1 = sem("h1_ready")
        s_h = sem("h_ready")
        s_carry = sem("carry_saved")
        s_hc = sem("hc_ready")
        s_y = sem("y_added")
        s_skip = sem("skip_ready")
        s_skip_y = sem("skip_added")
        s_y0 = sem("y0_saved")
        s_yt = sem("y_total_ready")
        s_low = sem("low_ranks_ready")
        s_high = sem("part_high_ready")
        s_lowr = sem("low_rows_copied")
        s_sub = sem("part_subtracted")
        s_mid = sem("part_mid_ready")
        s_parts = sem("parts_ready")
        s_dtp = sem("dt_projected")
        s_lin = sem("dt_linear_parts")
        s_abs = sem("dt_abs_ready")
        s_e = sem("dt_exp_ready")
        s_ln = sem("dt_log_ready")
        s_dt = sem("dt_ready")
        s_dtx = sem("dtx_ready")
        s_conv = sem("conv_ready")
        s_hid = sem("hidden_ready")
        s_xip = sem("xi_projected")
        s_zp = sem("z_projected")
        s_xia = sem("xi_ready")
        s_za = sem("z_ready")
        s_stat = [sem("norm1_stats"), sem("norm2_stats")]
        s_mom = [sem("norm1_moments"), sem("norm2_moments")]
        s_ve = [sem("norm1_var_eps"), sem("norm2_var_eps")]
        s_rstd = [sem("norm1_rstd"), sem("norm2_rstd")]
        s_shift = [sem("norm1_shift"), sem("norm2_shift")]
        s_norm = [sem("norm1_done"), sem("norm2_done")]
        s_t1 = sem("norm1_transposed")
        s_g = sem("norm1_affine_done")
        s_gz = sem("gated_ready")
        s_op = sem("out_projected")
        s_o = sem("out_projection_copied")
        s_t2 = sem("norm2_transposed")
        s_ot = sem("norm2_transposed_copied")
        s_fc2 = sem("fc2_ready")
        s_res = sem("result_ready")

        constants = [
            (ident[:, :], d["ident"]),
            (select_f32, d["select"].rearrange("r (j p) -> r j p", p=P)),
            (minus_f32, d["minus"].rearrange("r (i m) -> r i m", m=LOW)),
            (dw_all, d["dw_rep"].rearrange("p (t n) -> p t n", t=TAPS)),
            (fc1_t, d["fc1_t"]),
            (edge_w[:, :], d["edge_w"]),
            (edge_scale, d["edge_scale"]),
            (in_w[:, :, :], d["in_w_t"].rearrange("(a p) n -> p a n", p=P)),
            (in_b[:, :], d["in_b"]),
            (A[:, :, :, :], d["A_log"].rearrange("p (k a n) -> p k a n", k=DIRS, a=HALVES)),
            (D[:, :, :], d["Ds"].rearrange("p (k a) -> p k a", k=DIRS)),
            (norm1_w[:, :], d["norm1_w"]),
            (norm1_b[:, :], d["norm1_b"]),
            (norm2_w[:, :], d["norm2_w"]),
            (norm2_b[:, :], d["norm2_b"]),
            (out_w[:, :, :], d["out_w_t"].rearrange("(a p) n -> p a n", p=P)),
            (out_b[:, :], d["out_b"]),
            (fc2_w[:, :, :], d["fc2_w_t"].rearrange("(a p) n -> p a n", p=P)),
            (fc2_b_in, d["fc2_b"]),
        ]
        SETUP_DVE = 9

        block = ctx.enter_context(nc.Block())

        @block.sync
        def _(sp):
            for where, what in constants:
                sp.dma_start(where, what).then_inc(s_const, 16)

            def ahead(*values):
                for v in values:
                    if isinstance(v, bass.AP):
                        sp.lower_ap_dma(v)
                    elif not isinstance(v, int):
                        sp.lower_val(v)

            def load_pre(q, b, hw):
                top, bottom = hw == 0, hw == PRES - 1
                inner = x_halo[:, :, 1:W + 1]
                if top:
                    pieces = [(0, 1, None), (1, ROWS + 2, 0)]
                elif bottom:
                    pieces = [(ROWS + 1, ROWS + 2, None), (0, ROWS + 1, hw * ROWS - 1)]
                else:
                    pieces = [(0, 2, hw * ROWS - 1), (2, ROWS + 2, hw * ROWS + 1)]
                src = [d["zero_row"].rearrange("p (r w) -> p r w", r=1) if row is None
                       else d["x"][b, :, row:row + hi - lo, :] for lo, hi, row in pieces]
                ahead(q, *src)
                wait(sp, s_conv, q)
                if isinstance(q, int) and q == 0:
                    sp.wait_ge(s_setup_dve, SETUP_DVE)
                for (lo, hi, _), rows in zip(pieces, src):
                    sp.dma_start(inner[:, lo:hi, :], rows).then_inc(s_halo, 16)
                sp.dma_start(edge_rows[:, :], d["edge_rows"][hw]).then_inc(s_halo, 16)

            def store_pre(q, b, hw):
                tok = slice(hw * HALF, (hw + 1) * HALF)
                xi_to, z_to = xi_dram[b, :, :, tok], z_dram[b, :, :, tok]
                ahead(q + 1, xi_to, z_to)
                wait(sp, s_xia, q + 1)
                sp.dma_start(xi_to, xi_out[:, :, :]).then_inc(s_xi_st, 16)
                wait(sp, s_za, q + 1)
                sp.dma_start(z_to, z_out[:, :, :]).then_inc(s_z_st, 16)

            def load_window(s1, b, k, win, par, skips=0):
                src = xi_dram[b, :, :, win * WIN:(win + 1) * WIN]
                stored = 16 * (b * PRES + 2 * win + 2)
                ahead(skips, stored, s1 - 1, 2 * s1, 2 * (s1 - 1), src)
                wait(sp, s_skip, skips)
                wait(sp, s_xi_st, stored)
                wait(sp, s_dtx, 2 * (s1 - 1))
                wait(sp, s_low, s1 - 1)
                wait(sp, s_lin, 2 * s1)
                sp.dma_start(xi[par][:, :, :], src).then_inc(s_xi_in, 16)
                sp.dma_start(low_w[:, :, :], d["low_w"][k].rearrange("(a p) n -> p a n", p=P)).then_inc(s_xi_in, 16)
                sp.dma_start(dt_w[DT_AT:LOW, :], d["dt_w_t"][k]).then_inc(s_xi_in, 16)
                sp.dma_start(dt_b[:, :], d["dt_b"][k]).then_inc(s_xi_in, 16)

            def load_z(p, b, win):
                src = z_dram[b, :, :, win * WIN:(win + 1) * WIN]
                stored = 16 * (b * PRES + 2 * win + 2)
                ahead(2 * p, stored, src)
                wait(sp, s_gz, 2 * p)
                wait(sp, s_z_st, stored)
                sp.dma_start(z_in[:, :, :], src).then_inc(s_z_in, 16)

            def load_x(p, b, win):
                src = x_flat[b, :, win * WIN:(win + 1) * WIN]
                ahead(p, src)
                wait(sp, s_res, p)
                sp.dma_start(x_in[:, :], src).then_inc(s_x_in, 16)

            def store_out(p, b, win):
                to = out_flat[b, :, win * WIN:(win + 1) * WIN]
                ahead(p + 1, to)
                wait(sp, s_res, p + 1)
                sp.dma_start(to, result[:, :]).then_inc(s_out_st, 16)

            for hw in range(PRES):
                load_pre(hw, 0, hw)
                store_pre(hw, 0, hw)
            load_window(0, 0, 0, 0, 0)

            def image(b, first, last):
                for i in range(STEPS):
                    k, w = divmod(i, WINS)
                    s = b * STEPS + i
                    q = (b + 1) * PRES + i
                    skips = b * WINS + max(0, i - WINS)
                    if i + 1 < STEPS:
                        k1, w1 = divmod(i + 1, WINS)
                        load_window(s + 1, b, k1, w1 if k1 == 0 else WINS - 1 - w1, (i + 1) % 2, skips)
                    elif not last:
                        load_window(s + 1, b + 1, 0, 0, 0, skips)
                    if k == 1 and w >= 1:
                        load_z(b * WINS + w - 1, b, WINS - w)
                    if k == 1 and w >= 2:
                        load_x(b * WINS + w - 2, b, WINS + 1 - w)
                    if not first and i == 0:
                        load_z(b * WINS - 1, b - 1, 0)
                    if not first and i < 2:
                        load_x(b * WINS - 2 + i, b - 1, 1 - i)
                    if not last:
                        load_pre(q, b + 1, i)
                    if i == 0:
                        if not first:
                            store_pre(q - 1, b, PRES - 1)
                    elif not last:
                        store_pre(q - 1, b + 1, i - 1)
                    if k == 1 and w >= 2:
                        store_out(b * WINS + w - 2, b, WINS + 1 - w)
                    if not first and i < 2:
                        store_out(b * WINS - 2 + i, b - 1, 1 - i)

            image(0, True, False)
            with sp.Fori(1, IMAGES - 1) as b:
                image(b, False, False)
            image(IMAGES - 1, False, True)
            end = IMAGES * WINS
            load_z(end - 1, IMAGES - 1, 0)
            for p in (end - 2, end - 1):
                load_x(p, IMAGES - 1, end - 1 - p)
                store_out(p, IMAGES - 1, end - 1 - p)
            sp.wait_ge(s_xi_st, 16 * IMAGES * PRES)
            sp.wait_ge(s_z_st, 16 * IMAGES * PRES)
            sp.wait_ge(s_out_st, 16 * end)

        @block.tensor
        def _(pe):
            mm = nc.tensor.matmul

            def turn(out, in_, start):
                return mm(out, in_, ident[:, :], is_transpose=True, start=start, stop=True, skip_group_check=True)

            pe.wait_ge(s_const, 16 * len(constants))
            for a in range(HALVES):
                last = mm(post_bank[:, 0:1], fc2_w[:, a, :], norm2_b[:, a:a + 1], start=(a == 0), stop=(a == HALVES - 1))
            last.then_inc(s_setup_pe, 1)

            def conv(q, lo, hi):
                for i in range(lo, hi):
                    a, tap = divmod(i, TAPS + 1)
                    out = pre_bank[:, a * HALF:(a + 1) * HALF]
                    if tap < TAPS:
                        dy, dx = divmod(tap, 3)
                        last = mm(out, conv_w[:, tap, a * P:(a + 1) * P], x_halo[:, dy:dy + ROWS, dx:dx + W],
                                  start=(tap == 0), stop=False)
                    else:
                        last = mm(out, edge_w[:, a * P:(a + 1) * P], edge_rows[:, :], start=False, stop=True)
                if hi == HALVES * (TAPS + 1):
                    last.then_inc(s_conv, 1)

            def in_proj(bank, base, a, done):
                out = bank[:, a * HALF:(a + 1) * HALF]
                cols = slice(base + a * P, base + (a + 1) * P)
                for c in range(HALVES):
                    mm(out, in_w[:, c, cols], hidden[:, c, :], start=(c == 0), stop=False)
                last = mm(out, in_b[:, cols], ones[:, :], start=False, stop=True)
                if a == HALVES - 1:
                    last.then_inc(done, 1)

            def low_ranks(s1, par):
                pe.wait_ge(s_xi_in, 64 * (s1 + 1))
                for c in range(HALVES):
                    last = mm(pre_bank[0:LOW, :], low_w[:, c, :], xi[par][:, c, :], start=(c == 0), stop=(c == HALVES - 1))
                last.then_inc(s_low, 1)

            def subtract(s1, i):
                if i == 0:
                    pe.wait_ge(s_lowr, s1 + 1)
                    pe.wait_ge(s_high, s1 + 1)
                else:
                    pe.wait_ge(s_mid, s1 + 1)
                part = part_high if i == 0 else part_mid
                mm(pre_bank[0:LOW, :], minus[:, i, :], part[:, :], start=False, stop=True,
                   skip_group_check=True).then_inc(s_sub, 1)

            def dt_proj(s1, a):
                if a == 0:
                    pe.wait_ge(s_parts, s1 + 1)
                else:
                    pe.wait_ge(s_lin, 2 * s1 + 1)
                mm(pre_bank[:, :], dt_w[DT_AT:LOW, a * P:(a + 1) * P], low_rows[DT_AT:LOW, :],
                   start=True, stop=True).then_inc(s_dtp, 1)

            def spread_b(s, n, par):
                if n == 0:
                    pe.wait_ge(s_parts, s + 1)
                wait(pe, s_u0, s * STATES + n - 1)
                mm(b_bank[n % 2][:, :], select[:, n, :], parts[par][:, :], start=True, stop=True).then_inc(s_b, 1)

            def add_y(s, n, left, st):
                pe.wait_ge(s_hc, s * STATES + n + 1)
                if n == 0:
                    if left == 0:
                        pe.wait_ge(s_y0, st.kept_before + 1)
                    elif left == 1:
                        pe.wait_ge(s_yt, st.p1 + 1)
                for a in range(HALVES):
                    for j in range(BLOCKS):
                        last = turn(y_bank[:, j, a * P:(a + 1) * P], hc[:, n % RING, a, j * P:(j + 1) * P],
                                    start=(n == 0 and a == 0 and j % 2 == 0))
                last.then_inc(s_y, 1)

            def add_skip(count):
                pe.wait_ge(s_skip, count)
                for a in range(HALVES):
                    for j in range(BLOCKS):
                        last = turn(y_bank[:, j, a * P:(a + 1) * P], skip[:, a, j * P:(j + 1) * P], start=False)
                last.then_inc(s_skip_y, 1)

            def turn1(p, a):
                if a == 0:
                    pe.wait_ge(s_norm[0], p + 1)
                else:
                    pe.wait_ge(s_g, 2 * p + 1)
                for j in range(BLOCKS):
                    last = turn(post_bank[:, j * P:(j + 1) * P], yt[:, j, a * P:(a + 1) * P], start=True)
                last.then_inc(s_t1, 1)

            def out_proj(p, a):
                if a == 0:
                    pe.wait_ge(s_gz, 2 * p + 2)
                else:
                    pe.wait_ge(s_o, 2 * p + 1)
                for jj in range(2):
                    j = 2 * a + jj
                    out = post_bank[:, jj * INNER:(jj + 1) * INNER]
                    for c in range(HALVES):
                        mm(out, gated[:, c, j * P:(j + 1) * P], out_w[:, c, :], start=(c == 0), stop=False)
                    last = mm(out, ones[:, 0:P], out_b[:, :], start=False, stop=True)
                last.then_inc(s_op, 1)

            def turn2(p, a):
                if a == 0:
                    pe.wait_ge(s_norm[1], p + 1)
                else:
                    pe.wait_ge(s_ot, 2 * p + 1)
                for j in range(BLOCKS):
                    last = turn(post_bank[:, j * P:(j + 1) * P], o[:, j, a * P:(a + 1) * P], start=True)
                last.then_inc(s_t2, 1)

            def fc2(p):
                pe.wait_ge(s_ot, 2 * p + 2)
                for c in range(HALVES):
                    last = mm(post_bank[:, :], fc2_w[:, c, :], o_t[:, c, :], start=(c == 0), stop=(c == HALVES - 1))
                last.then_inc(s_fc2, 1)

            pe.wait_ge(s_setup_dve, SETUP_DVE)
            pe.wait_ge(s_setup_act, 3)
            def pre_alone(q):
                pe.wait_ge(s_halo, 48 * (q + 1))
                wait(pe, s_xia, q)
                conv(q, 0, HALVES * (TAPS + 1))
                pe.wait_ge(s_hid, q + 1)
                for a in range(HALVES):
                    in_proj(pre_bank, 0, a, s_xip)
                wait(pe, s_za, q)
                for a in range(HALVES):
                    in_proj(post_bank, INNER, a, s_zp)

            pre_alone(0)
            with pe.Fori(1, PRES) as q:
                pre_alone(q)
            pe.wait_ge(s_xia, PRES)
            pe.wait_ge(s_za, PRES)
            low_ranks(0, 0)
            subtract(0, 0)
            subtract(0, 1)
            dt_proj(0, 0)
            dt_proj(0, 1)
            spread_b(0, 0, 0)

            def step(st):
                s, par, nxt = st.s, st.parity, 1 - st.parity
                for n in range(STATES):
                    if n + 1 < STATES:
                        spread_b(s, n + 1, par)
                    elif not st.last:
                        spread_b(s + 1, 0, nxt)
                    if n == 3 and st.post2:
                        out_proj(st.p2, 1)
                    if n >= LAG:
                        add_y(s, n - LAG, st.left, st)
                    elif not st.first:
                        add_y(s - 1, STATES - LAG + n, None, st)
                    if n == 6 and st.k == 1:
                        add_skip(st.b * WINS + st.w + 1)
                    if not st.last:
                        if n == 1:
                            if st.finish:
                                pe.wait_ge(s_xia, st.pre_index)
                            low_ranks(s + 1, nxt)
                        if n in (2, 3):
                            subtract(s + 1, n - 2)
                        if n in (4, 5):
                            dt_proj(s + 1, n - 4)
                    if st.pre:
                        if n == CONV_SLOTS[0]:
                            pe.wait_ge(s_halo, 48 * (st.pre_index + 1))
                            pe.wait_ge(s_lin, 2 * (s + 1) + 2)
                        if n in CONV_SLOTS:
                            i = n - CONV_SLOTS[0]
                            conv(st.pre_index, CONV_CUTS[i], CONV_CUTS[i + 1])
                        if n == 14:
                            pe.wait_ge(s_hid, st.pre_index + 1)
                            for a in range(HALVES):
                                in_proj(pre_bank, 0, a, s_xip)
                    if st.post2:
                        if n == 2:
                            if st.finish:
                                pe.wait_ge(s_za, st.pre_index)
                            out_proj(st.p2, 0)
                        if n == 8:
                            pe.wait_ge(s_o, 2 * st.p2 + 2)
                            turn2(st.p2, 0)
                        if n == 9:
                            turn2(st.p2, 1)
                        if n == 10:
                            fc2(st.p2)
                    if st.post1:
                        if n == 12:
                            if st.post2:
                                pe.wait_ge(s_res, st.p2 + 1)
                            elif st.finish:
                                pe.wait_ge(s_za, st.pre_index)
                            turn1(st.p1, 0)
                        if n == 13:
                            turn1(st.p1, 1)
                    if st.pre and n == 15:
                        if st.post1:
                            pe.wait_ge(s_g, 2 * st.p1 + 2)
                        elif st.post2:
                            pe.wait_ge(s_res, st.p2 + 1)
                        wait(pe, s_za, st.pre_index)
                        for a in range(HALVES):
                            in_proj(post_bank, INNER, a, s_zp)

            walk(pe, step)
            end = IMAGES * WINS
            s_end = IMAGES * STEPS
            for n in range(STATES - LAG, STATES):
                add_y(s_end - 1, n, None, None)
            for p in (end - 2, end - 1):
                if p == end - 1:
                    pe.wait_ge(s_res, p)
                    turn1(p, 0)
                    turn1(p, 1)
                for a in range(2):
                    out_proj(p, a)
                pe.wait_ge(s_o, 2 * p + 2)
                turn2(p, 0)
                turn2(p, 1)
                fc2(p)

        @block.scalar
        def _(act):
            run = nc.scalar.activation
            nc.scalar.preload_act_table_set(LN_EXP_SET)
            act.wait_ge(s_const, 16 * len(constants))
            run(A[:, :, :, :], A[:, :, :, :], ACT.Exp).then_inc(s_setup_act, 1)
            nc.scalar.copy(select[:, :, :], select_f32).then_inc(s_setup_act, 1)
            nc.scalar.copy(minus[:, :, :], minus_f32).then_inc(s_setup_act, 1)

            def silu_hidden(q):
                act.wait_ge(s_conv, q + 1)
                run(hidden[:, :, :], pre_bank[:, :].rearrange("p (a n) -> p a n", a=HALVES), ACT.Silu).then_inc(s_hid, 1)

            def silu_xi_z(q):
                act.wait_ge(s_xip, q + 1)
                wait(act, s_xi_st, 16 * q)
                run(xi_out[:, :, :], pre_bank[:, :].rearrange("p (a n) -> p a n", a=HALVES), ACT.Silu).then_inc(s_xia, 1)
                act.wait_ge(s_zp, q + 1)
                wait(act, s_z_st, 16 * q)
                run(z_out[:, :, :], post_bank[:, :].rearrange("p (a n) -> p a n", a=HALVES), ACT.Silu).then_inc(s_za, 1)

            def split_high(s1, par):
                act.wait_ge(s_low, s1 + 1)
                wait(act, s_cst, 16 * s1)
                wait(act, s_dtp, 2 * s1)
                nc.scalar.copy(low_rows[C_AT:LOW, :], pre_bank[C_AT:LOW, :]).then_inc(s_lowr, 1)
                wait(act, s_sub, 2 * s1)
                nc.scalar.copy(part_high[:, :], pre_bank[0:SPREAD, :]).then_inc(s_high, 1)
                act.wait_ge(s_lowr, s1 + 1)
                for i in range(C_PAIRS):
                    wait(act, s_c[i], 32 * (s1 - 1))
                nc.scalar.dma_start(c_dram[par], low_rows[C_AT:C_AT + STATES, :]).then_inc(s_cst, 16)

            def split_mid(s1):
                act.wait_ge(s_sub, 2 * s1 + 1)
                nc.scalar.copy(part_mid[:, :], pre_bank[0:SPREAD, :]).then_inc(s_mid, 1)

            def split_low(s1, par):
                act.wait_ge(s_sub, 2 * s1 + 2)
                nc.scalar.copy(parts[par][:, :], pre_bank[0:SPREAD, :]).then_inc(s_parts, 1)

            def load_c(s1, par, m):
                act.wait_ge(s_cst, 16 * (s1 + 1))
                wait(act, s_hc, s1 * STATES + 2 * m + 2 - C_RING)
                at = 2 * (m % C_PAIRS)
                src = c_dram[par:par + 1, 2 * m:2 * m + 2, :].broadcast_to((P, 2, WIN))
                nc.scalar.dma_start(c_rows[:, at:at + 2, :], src).then_inc(s_c[m % C_PAIRS], 16)

            def dt_linear(s1, a):
                act.wait_ge(s_dtp, 2 * s1 + a + 1)
                if a == 0:
                    wait(act, s_dt, s1)
                run(dt_exp[:, a, :], pre_bank[:, :], ACT.Abs, bias=dt_b[:, a:a + 1]).then_inc(s_abs, 1)
                run(dt_lin[:, a, :], pre_bank[:, :], ACT.Relu, bias=dt_b[:, a:a + 1]).then_inc(s_lin, 1)

            def dt_softplus(s1):
                act.wait_ge(s_abs, 2 * s1 + 2)
                run(dt_exp[:, :, :], dt_exp[:, :, :], ACT.Exp, scale=-1.0).then_inc(s_e, 1)
                act.wait_ge(s_e, s1 + 1)
                run(dt_exp[:, :, :], dt_exp[:, :, :], ACT.Ln, bias=1.0).then_inc(s_ln, 1)

            def decays(st, n):
                s = st.s
                if n == 0:
                    act.wait_ge(s_dt, s + 1)
                wait(act, s_h, s * STATES + n - RING + 1)
                for a in range(HALVES):
                    last = run(decay[:, n % RING, a, :], dt[st.parity][:, a, :], ACT.Exp, scale=A[:, st.k, a, n:n + 1])
                last.then_inc(s_decay, 1)

            def affine1(p, a):
                act.wait_ge(s_t1, 2 * p + a + 1)
                run(gated[:, a, :], post_bank[:, :], ACT.Identity, bias=norm1_b[:, a:a + 1],
                    scale=norm1_w[:, a:a + 1]).then_inc(s_g, 1)

            def copy_o(p, a):
                act.wait_ge(s_op, 2 * p + a + 1)
                nc.scalar.copy(o[:, 2 * a:2 * a + 2, :], post_bank[:, :].rearrange("p (j n) -> p j n", j=2)).then_inc(s_o, 1)

            def copy_ot(p, a):
                act.wait_ge(s_t2, 2 * p + a + 1)
                if a == 0:
                    wait(act, s_fc2, p)
                nc.scalar.copy(o_t[:, a, :], post_bank[:, :]).then_inc(s_ot, 1)

            def normalize(i, buf, p):
                act.wait_ge(s_shift[i], p + 1)
                for j in range(BLOCKS):
                    last = run(buf[:, j, :], buf[:, j, :], ACT.Identity, bias=shift[i][:, j:j + 1], scale=rstd[i][:, j:j + 1])
                last.then_inc(s_norm[i], 1)

            nc.scalar.preload_act_table_set(SILU_SET)
            silu_hidden(0)
            silu_xi_z(0)
            with act.Fori(1, PRES) as q:
                silu_hidden(q)
                silu_xi_z(q)
            nc.scalar.preload_act_table_set(LN_EXP_SET)
            act.wait_ge(s_setup_dve, SETUP_DVE)
            split_high(0, 0)
            split_mid(0)
            split_low(0, 0)
            load_c(0, 0, 0)
            dt_linear(0, 0)
            dt_linear(0, 1)
            dt_softplus(0)

            def step(st):
                s, par, nxt = st.s, st.parity, 1 - st.parity
                decays(st, 0)
                decays(st, 1)
                for n in range(STATES):
                    if n + 2 < STATES:
                        decays(st, n + 2)
                    if n % 2 == 0:
                        m = n // 2 + 1
                        if m < STATES // 2:
                            load_c(s, par, m)
                        elif not st.last:
                            load_c(s + 1, nxt, m - STATES // 2)
                    if n == 0 and st.finish:
                        nc.scalar.preload_act_table_set(SILU_SET)
                        silu_xi_z(st.pre_index - 1)
                        nc.scalar.preload_act_table_set(LN_EXP_SET)
                    if n == 2 and st.keep_y0:
                        act.wait_ge(s_y, s * STATES)
                        wait(act, s_yt, st.b * WINS)
                        nc.scalar.copy(y0[:, blocks_of(st.keep_window), :], y_bank[:, :, :]).then_inc(s_y0, 1)
                    if n in (2, 3) and st.post2:
                        copy_o(st.p2, n - 2)
                    if not st.last:
                        if n == 1:
                            split_high(s + 1, nxt)
                        if n == 2:
                            split_mid(s + 1)
                        if n == 3:
                            split_low(s + 1, nxt)
                        if n == 4:
                            dt_linear(s + 1, 0)
                        if n == 5:
                            dt_linear(s + 1, 1)
                        if n == 6:
                            dt_softplus(s + 1)
                    if n == 4 and st.k == 1:
                        wait(act, s_skip_y, st.b * WINS + st.w)
                        act.wait_ge(s_xi_in, 64 * (s + 1))
                        for a in range(HALVES):
                            last = run(skip[:, a, :], xi[par][:, a, :], ACT.Copy, scale=D_sum[:, a:a + 1])
                        last.then_inc(s_skip, 1)
                    if st.post2:
                        if n == 7:
                            normalize(1, o, st.p2)
                        if n == 8:
                            copy_ot(st.p2, 0)
                        if n == 9:
                            copy_ot(st.p2, 1)
                    if st.post1 and n == 10:
                        normalize(0, yt, st.p1)
                    if st.post1 and n == 12:
                        affine1(st.p1, 0)
                    if st.pre and n == 13:
                        nc.scalar.preload_act_table_set(SILU_SET)
                        silu_hidden(st.pre_index)
                        nc.scalar.preload_act_table_set(LN_EXP_SET)
                    if st.post1 and n == 13:
                        affine1(st.p1, 1)

            walk(act, step)
            end = IMAGES * WINS
            normalize(0, yt, end - 1)
            for p in (end - 2, end - 1):
                if p == end - 1:
                    affine1(p, 0)
                    affine1(p, 1)
                copy_o(p, 0)
                copy_o(p, 1)
                normalize(1, o, p)
                copy_ot(p, 0)
                copy_ot(p, 1)

        @block.vector
        def _(dve):
            V = nc.vector
            dve.wait_ge(s_const, 16 * len(constants))
            V.memset(x_halo[:, :, :], 0.0).then_inc(s_setup_dve, 1)
            V.memset(ones[:, :], 1.0).then_inc(s_setup_dve, 1)
            V.memset(minus_half[:, :], -0.5).then_inc(s_setup_dve, 1)
            V.tensor_tensor(conv_w[:, :, :], dw_all, fc1_t.rearrange("p (t n) -> p t n", t=1).broadcast_to((P, TAPS, INNER)),
                            ALU.mult).then_inc(s_setup_dve, 1)
            V.tensor_tensor(edge_w[:, :], edge_w[:, :], edge_scale, ALU.mult).then_inc(s_setup_dve, 1)
            V.tensor_tensor(D_sum[:, :], D[:, 0, :], D[:, 1, :], ALU.add).then_inc(s_setup_dve, 1)
            dve.wait_ge(s_setup_act, 1)
            V.tensor_scalar(A[:, :, :, :], A[:, :, :, :], -1.0, None, ALU.mult).then_inc(s_setup_dve, 1)
            dve.wait_ge(s_setup_pe, 1)
            V.tensor_tensor(fc2_b[:, :], post_bank[:, 0:1], fc2_b_in, ALU.add).then_inc(s_setup_dve, 1)
            V.tensor_tensor(fc2_w[:, :, :], fc2_w[:, :, :],
                            norm2_w[:, :].rearrange("p (a n) -> p a n", n=1).broadcast_to((P, HALVES, DIM)),
                            ALU.mult).then_inc(s_setup_dve, 1)
            dve.wait_ge(s_setup_dve, SETUP_DVE)

            def dt_sum(s1, par):
                dve.wait_ge(s_ln, s1 + 1)
                dve.wait_ge(s_lin, 2 * s1 + 2)
                V.tensor_tensor(dt[par][:, :, :], dt_exp[:, :, :], dt_lin[:, :, :], ALU.add).then_inc(s_dt, 1)

            def norm_stats(i, src, p):
                for j in range(BLOCKS):
                    V.bn_stats(stats[i][:, j, :], src[:, j, :]).then_inc(s_stat[i], 1)

            def norm_moments(i, p):
                dve.wait_ge(s_stat[i], BLOCKS * (p + 1))
                V.memset(var_eps[i][:, :], EPS).then_inc(s_ve[i], 1)
                for j in range(BLOCKS):
                    V.bn_aggr(moments[i][:, j, :], stats[i][:, j, :]).then_inc(s_mom[i], 1)

            def norm_var(i, p):
                dve.wait_ge(s_ve[i], 2 * p + 1)
                dve.wait_ge(s_mom[i], BLOCKS * (p + 1))
                V.tensor_tensor(var_eps[i][:, :], var_eps[i][:, :], moments[i][:, :, 1], ALU.add).then_inc(s_ve[i], 1)

            def norm_shift(i, p):
                dve.wait_ge(s_rstd[i], p + 1)
                wait(dve, s_norm[i], p)
                V.scalar_tensor_tensor(out=shift[i][:, :], in0=moments[i][:, :, 0], scalar=-1.0, in1=rstd[i][:, :],
                                       op0=ALU.mult, op1=ALU.mult).then_inc(s_shift[i], 1)

            def total_y(s, p, window):
                dve.wait_ge(s_y, s * STATES)
                dve.wait_ge(s_skip_y, p + 1)
                wait(dve, s_t1, 2 * p)
                dve.wait_ge(s_y0, p + 1)
                V.tensor_tensor(yt[:, :, :], y_bank[:, :, :], y0[:, blocks_of(window), :],
                                ALU.add).then_inc(s_yt, 1)

            def finish_out(p):
                dve.wait_ge(s_fc2, p + 1)
                dve.wait_ge(s_x_in, 16 * (p + 1))
                wait(dve, s_out_st, 16 * p)
                V.scalar_tensor_tensor(out=result[:, :], in0=post_bank[:, :], scalar=fc2_b[:, 0:1], in1=x_in[:, :],
                                       op0=ALU.add, op1=ALU.add).then_inc(s_res, 1)

            dt_sum(0, 0)

            def step(st):
                s, par, nxt, k = st.s, st.parity, 1 - st.parity, st.k
                way = slice(None) if k == 0 else slice(WIN - 1, None, -1)
                end = WIN - 1 if k == 0 else 0

                def make_u(n, a, done):
                    V.tensor_tensor(u_bank[a][:, :], dtx[par][:, a, :], b_bank[n % 2][:, :], ALU.mult).then_inc(done, 1)

                def scan(n, a, done):
                    V.tensor_tensor_scan(h[:, n % RING, a, way], decay[:, n % RING, a, way], u_bank[a][:, way],
                                         0.0 if st.static_w == 0 else carry[:, n, a:a + 1],
                                         ALU.mult, ALU.add).then_inc(done, 1)

                def keep_carry(n, step_of):
                    dve.wait_ge(s_h, step_of * STATES + n + 1)
                    V.tensor_copy(carry[:, n - RING + 1:n + 1, :], h[:, :, :, end]).then_inc(s_carry, 1)

                kept = s * (STATES // RING - 1) + (st.b * DIRS + k) * (WINS - 1) + st.w
                for n in range(STATES):
                    count = s * STATES + n
                    if n == 0:
                        dve.wait_ge(s_dtx, HALVES * (s + 1))
                    dve.wait_ge(s_b, count + 1)
                    wait(dve, s_h1, count)
                    make_u(n, 1, s_u1)
                    wait(dve, s_h, count)
                    if n == 0 and st.static_w != 0:
                        keep_carry(STATES - 1, s - 1)
                    if n and n % RING == 0:
                        keep_carry(n - 1, s)
                    make_u(n, 0, s_u0)
                    if n == 8 and not st.last:
                        dt_sum(s + 1, nxt)
                    if st.post2:
                        if n == 5:
                            norm_moments(1, st.p2)
                        if n == 7:
                            norm_shift(1, st.p2)
                    if st.post1:
                        if n == 4:
                            norm_moments(0, st.p1)
                        if n == 6:
                            norm_shift(0, st.p1)
                    dve.wait_ge(s_u1, count + 1)
                    dve.wait_ge(s_decay, count + 1)
                    wait(dve, s_hc, count - RING + 1)
                    wait(dve, s_carry, kept + n // RING)
                    scan(n, 1, s_h1)
                    dve.wait_ge(s_u0, count + 1)
                    scan(n, 0, s_h)
                    if st.post1:
                        if n == 2:
                            total_y(s, st.p1, st.p1_window)
                        if n == 3:
                            dve.wait_ge(s_yt, st.p1 + 1)
                            norm_stats(0, yt, st.p1)
                        if n == 4:
                            norm_var(0, st.p1)
                    if st.post2:
                        if n == 4:
                            dve.wait_ge(s_o, 2 * st.p2 + 2)
                            norm_stats(1, o, st.p2)
                        if n == 5:
                            norm_var(1, st.p2)
                        if n == 11:
                            finish_out(st.p2)

            walk(dve, step)
            end = IMAGES * WINS
            total_y(IMAGES * STEPS, end - 1, 0)
            dve.wait_ge(s_yt, end)
            norm_stats(0, yt, end - 1)
            norm_moments(0, end - 1)
            norm_var(0, end - 1)
            norm_shift(0, end - 1)
            for p in (end - 2, end - 1):
                dve.wait_ge(s_o, 2 * p + 2)
                norm_stats(1, o, p)
                norm_moments(1, p)
                norm_var(1, p)
                norm_shift(1, p)
                finish_out(p)

        @block.gpsimd
        def _(pool):
            G = nc.gpsimd

            def inverse_root(i, p):
                pool.wait_ge(s_ve[i], 2 * p + 2)
                G.tensor_tensor(rstd[i][:, :], var_eps[i][:, :], minus_half[:, :], ALU.pow).then_inc(s_rstd[i], 1)

            def gate(p, a):
                pool.wait_ge(s_g, 2 * p + 1 + a)
                pool.wait_ge(s_z_in, 16 * (p + 1))
                G.tensor_tensor(gated[:, a, :], gated[:, a, :], z_in[:, a, :], ALU.mult).then_inc(s_gz, 1)

            def dt_times_x(s1, par, a):
                if a == 0:
                    pool.wait_ge(s_xi_in, 64 * (s1 + 1))
                    pool.wait_ge(s_dt, s1 + 1)
                G.tensor_tensor(dtx[par][:, a, :], dt[par][:, a, :], xi[par][:, a, :], ALU.mult).then_inc(s_dtx, 1)

            pool.wait_ge(s_setup_dve, SETUP_DVE)
            for a in range(HALVES):
                dt_times_x(0, 0, a)

            def step(st):
                for n in range(STATES):
                    count = st.s * STATES + n
                    pool.wait_ge(s_h, count + 1)
                    if n % 2 == 0:
                        pool.wait_ge(s_c[n // 2 % C_PAIRS], 16 * (2 * st.s + n // C_RING + 1))
                    wait(pool, s_y, count - RING + 1)
                    G.tensor_tensor(hc[:, n % RING, :, :], h[:, n % RING, :, :],
                                    c_rows[:, n % C_RING, :].rearrange("p (a n) -> p a n", a=1).broadcast_to((P, HALVES, WIN)),
                                    ALU.mult).then_inc(s_hc, 1)
                    if st.post1 and n == 4:
                        inverse_root(0, st.p1)
                    if st.post2 and n == 5:
                        inverse_root(1, st.p2)
                    if not st.last and n in (9, 10):
                        dt_times_x(st.s + 1, 1 - st.parity, n - 9)
                    if st.post1 and n in (13, 14):
                        gate(st.p1, n - 13)

            walk(pool, step)
            end = IMAGES * WINS
            inverse_root(0, end - 1)
            for p in (end - 2, end - 1):
                if p == end - 1:
                    gate(p, 0)
                    gate(p, 1)
                inverse_root(1, p)


def edge_table():
    inside = np.ones((PRES, TAPS + 1, ROWS, W), np.float32)
    for tap in range(TAPS):
        dy, dx = divmod(tap, 3)
        if dy == 0:
            inside[0, tap, 0, :] = 0
        if dy == 2:
            inside[PRES - 1, tap, ROWS - 1, :] = 0
        if dx == 0:
            inside[:, tap, :, 0] = 0
        if dx == 2:
            inside[:, tap, :, W - 1] = 0
    return inside.reshape(PRES, TAPS + 1, HALF)


def select_table():
    table = np.zeros((SPREAD, STATES, P), np.float32)
    for r in range(SPREAD):
        table[r, r % STATES, :] = 1
    return table.reshape(SPREAD, STATES * P)


def minus_table():
    table = np.zeros((SPREAD, 2, LOW), np.float32)
    for i in range(2):
        for r in range((i + 1) * STATES, SPREAD):
            table[r, i, r] = -1
    return table.reshape(SPREAD, 2 * LOW)


def kernel(**inputs):
    import concourse.bacc as bacc
    from concourse.bass_utils import run_bass_kernel_spmd

    get = {n.removeprefix("L0_conv_"): np.asarray(a) for n, a in inputs.items()}
    xw = get["x_proj_w"]
    B, C = xw[:, RANK:RANK + STATES, :], xw[:, RANK + STATES:, :]
    gap = np.zeros((DIRS, C_AT - SPREAD, INNER), np.float32)
    one_row = np.ones((1, INNER), np.float32)
    arrays = {
        "x": get["x"],
        "ident": np.eye(P, dtype=np.float32),
        "select": select_table(),
        "minus": minus_table(),
        "edge_rows": edge_table(),
        "zero_row": np.zeros((P, W), np.float32),
        "fc1_t": get["fc1_w"].T,
        "dw_rep": np.broadcast_to(get["dw_w"].reshape(INNER, TAPS).T.reshape(1, TAPS * INNER), (P, TAPS * INNER)),
        "edge_w": np.concatenate([get["dw_w"].reshape(INNER, TAPS).T, get["dw_b"].reshape(1, INNER)]),
        "edge_scale": np.concatenate([np.broadcast_to(get["fc1_b"].reshape(1, INNER), (TAPS, INNER)), one_row]),
        "in_w_t": get["in_proj_w"].T,
        "in_b": get["in_proj_b"].reshape(1, 2 * INNER),
        "low_w": np.concatenate([B, B, B, gap, C, gap, xw[:, :RANK, :]], axis=1).transpose(0, 2, 1),
        "dt_w_t": get["dt_proj_w"].transpose(0, 2, 1),
        "dt_b": get["dt_proj_b"].reshape(DIRS, HALVES, P).transpose(0, 2, 1),
        "A_log": get["A_log"].reshape(DIRS, HALVES, P, STATES).transpose(2, 0, 1, 3).reshape(P, -1),
        "Ds": get["Ds"].reshape(DIRS, HALVES, P).transpose(2, 0, 1).reshape(P, -1),
        "norm1_w": get["out_norm_w"].reshape(HALVES, P).T,
        "norm1_b": get["out_norm_b"].reshape(HALVES, P).T,
        "norm2_w": get["norm_w"].reshape(HALVES, P).T,
        "norm2_b": get["norm_b"].reshape(HALVES, P).T,
        "out_w_t": get["out_proj_w"].T,
        "out_b": get["out_proj_b"].reshape(1, INNER),
        "fc2_w_t": get["fc2_w"].T,
        "fc2_b": get["fc2_b"].reshape(DIM, 1),
    }
    nc = bacc.Bacc("TRN2", target_bir_lowering=False, num_devices=1)
    feed, d = {}, {}
    for name, a in arrays.items():
        a = np.ascontiguousarray(a)
        feed[f"in_{name}"] = a
        d[name] = nc.dram_tensor(f"in_{name}", a.shape, mybir.dt.from_np(a.dtype), kind="ExternalInput").ap()
    d["out"] = nc.dram_tensor("out_0", (IMAGES, DIM, H, W), F32, kind="ExternalOutput").ap()
    build(nc, d)
    r = run_bass_kernel_spmd(nc, [feed], core_ids=[0])
    return r.results[0]["out_0"]
```

```python
from contextlib import ExitStack

import numpy as np

import concourse.bass as bass
from concourse import mybir

ALU = mybir.AluOpType
ACT = mybir.ActivationFunctionType
F32 = mybir.dt.float32
BF16 = mybir.dt.bfloat16

IMAGES, DIM, H, W = 16, 128, 64, 64
P = 128
INNER, STATES, RANK, DIRS = 256, 16, 16, 2
HALVES = INNER // P
TOKENS = H * W
WIN = 512
WINS = TOKENS // WIN
BLOCKS = WIN // P
HALF = WIN // 2
PRES = TOKENS // HALF
ROWS = HALF // W
STEPS = DIRS * WINS
TAPS = 9
PARTS = 3
SPREAD = PARTS * STATES
C_AT, DT_AT = 64, 96
LOW = DT_AT + RANK
EPS = 1e-6
RING = 4
LAG = 3
CONV_SLOTS = range(7, 12)
CONV_CUTS = (0, 5, 10, 14, 17, 20)
C_PAIRS = 4
C_RING = 2 * C_PAIRS
LN_EXP_SET = "natural_log_exp_and_others"
SILU_SET = "silu_and_others"


class Step:

    def __init__(self, b, k, w, parity, first_image, last_image):
        self.b, self.k, self.w, self.parity = b, k, w, parity
        self.s = b * STEPS + k * WINS + w
        self.static_w = w if isinstance(w, int) else None
        w0 = self.static_w
        self.first = first_image and k == 0 and w0 == 0
        self.last = last_image and k == 1 and w0 == WINS - 1
        self.pre = not last_image
        self.pre_index = (b + 1) * PRES + k * WINS + w
        if self.first:
            self.finish = False
        elif last_image:
            self.finish = k == 0 and w0 == 0
        else:
            self.finish = True
        if w0 == 0:
            self.left = None if self.first else (1 - k)
        else:
            self.left = k
        self.keep_y0 = self.left == 0
        self.keep_window = WINS - 1 if (k == 1 and w0 == 0) else w - 1
        self.kept_before = b * WINS + self.keep_window
        if k == 1:
            self.post1 = w0 is None or w0 >= 1
            self.post2 = w0 is None or w0 >= 2
            self.p1 = b * WINS + w - 1
            self.p2 = b * WINS + w - 2
            self.p1_window, self.p2_window = w * -1 + WINS, w * -1 + (WINS + 1)
        else:
            self.post1 = w0 == 0 and not first_image
            self.post2 = w0 in (0, 1) and not first_image
            self.p1 = b * WINS - 1
            self.p1_window = 0
            self.p2 = b * WINS - 2 + w
            self.p2_window = 1 - w if w0 in (0, 1) else 0


def walk(engine, do_step):

    def image(b, first, last):
        for k in range(DIRS):
            head = WINS if first and k == 1 else 2
            for w in range(head):
                do_step(Step(b, k, w, w % 2, first, last))
            if head < WINS:
                with engine.Fori(1, WINS // 2 - 1) as j:
                    for par in range(2):
                        do_step(Step(b, k, 2 * j + par, par, first, last))
                for w in range(WINS - 2, WINS):
                    do_step(Step(b, k, w, w % 2, first, last))

    image(0, True, False)
    with engine.Fori(1, IMAGES - 1) as b:
        image(b, False, False)
    image(IMAGES - 1, False, True)


def halo_count(q, par):
    return q * 24 + (48 - 24 * par)


def blocks_of(window):
    if isinstance(window, int):
        return slice(window * BLOCKS, (window + 1) * BLOCKS)
    return bass.ds(window * BLOCKS, BLOCKS)


def wait(engine, sem, value):
    if isinstance(value, int) and value <= 0:
        return
    engine.wait_ge(sem, value)


def build(nc, d):
    ctx = ExitStack()
    with ctx:
        def sb(name, shape, dt=F32):
            return ctx.enter_context(nc.sbuf_tensor(name, shape, dt))

        def ps(name, shape):
            return ctx.enter_context(nc.psum_tensor(name, shape, F32))

        def sem(name):
            return ctx.enter_context(nc.semaphore(name))

        x_flat = d["x"].rearrange("b c h w -> b c (h w)")
        out_flat = d["out"].rearrange("b c h w -> b c (h w)")
        c_dram = nc.dram_tensor("c_scratch", (2, STATES, WIN), F32, kind="Internal").ap()
        xi_dram = nc.dram_tensor("xi_scratch", (IMAGES, P, HALVES, TOKENS), F32, kind="Internal").ap()
        z_dram = nc.dram_tensor("z_scratch", (IMAGES, P, HALVES, TOKENS), F32, kind="Internal").ap()

        ident = sb("ident", [P, P])
        select = sb("select", [SPREAD, STATES, P], BF16)
        minus = sb("minus", [SPREAD, 2, LOW], BF16)
        conv_w = sb("conv_w", [P, TAPS, INNER])
        edge_w = sb("edge_w", [TAPS + 1, INNER])
        in_w = sb("in_w", [P, HALVES, 2 * INNER])
        in_b = sb("in_b", [P, 2, HALVES])
        ones = sb("ones", [1, P])
        low_w = sb("low_w", [P, HALVES, LOW])
        dt_w = sb("dt_w", [LOW, INNER])
        dt_b = sb("dt_b", [P, HALVES])
        A = sb("A", [P, DIRS, HALVES, STATES])
        D = sb("D", [P, DIRS, HALVES])
        D_sum = sb("D_sum", [P, HALVES])
        norm1_w = sb("norm1_w", [P, HALVES])
        norm1_b = sb("norm1_b", [P, HALVES])
        norm2_w = sb("norm2_w", [P, HALVES])
        norm2_b = sb("norm2_b", [P, HALVES])
        out_w = sb("out_w", [P, HALVES, INNER])
        out_b = sb("out_b", [1, INNER])
        fc2_w = sb("fc2_w", [P, HALVES, DIM])
        fc2_b = sb("fc2_b", [P, 1])
        minus_half = sb("minus_half", [P, BLOCKS])

        x_halo = [sb(f"x_halo{i}", [P, ROWS + 2, W + 2]) for i in range(2)]
        edge_rows = [sb(f"edge_rows{i}", [TAPS + 1, HALF]) for i in range(2)]
        hidden = sb("hidden", [P, HALVES, HALF])
        xi_out = sb("xi_out", [P, HALVES, HALF])
        z_out = sb("z_out", [P, HALVES, HALF])
        xi = [sb(f"xi{i}", [P, HALVES, WIN]) for i in range(2)]
        dt = [sb(f"dt{i}", [P, HALVES, WIN]) for i in range(2)]
        dtx = [sb(f"dtx{i}", [P, HALVES, WIN]) for i in range(2)]
        parts = [sb(f"parts{i}", [SPREAD, WIN], BF16) for i in range(2)]
        part_high = sb("part_high", [SPREAD, WIN], BF16)
        part_mid = sb("part_mid", [SPREAD, WIN], BF16)
        low_rows = sb("low_rows", [LOW, WIN])
        dt_lin = sb("dt_lin", [P, HALVES, WIN])
        dt_exp = sb("dt_exp", [P, HALVES, WIN])
        skip = sb("skip", [P, HALVES, WIN])
        decay = sb("decay", [P, RING, HALVES, WIN])
        c_rows = sb("c_rows", [P, C_RING, WIN])
        h = sb("h", [P, RING, HALVES, WIN])
        hc = sb("hc", [P, RING, HALVES, WIN])
        carry = sb("carry", [P, STATES, HALVES])
        y0 = sb("y0", [P, TOKENS // P, INNER])
        yt = sb("yt", [P, BLOCKS, INNER])
        gated = sb("gated", [P, HALVES, WIN])
        z_in = sb("z_in", [P, HALVES, WIN])
        o = sb("o", [P, BLOCKS, INNER])
        o_t = sb("o_t", [P, HALVES, WIN])
        x_in = sb("x_in", [P, WIN])
        result = sb("result", [P, WIN])
        stats = [sb(f"stats{i}", [P, BLOCKS, 6]) for i in range(2)]
        moments = [sb(f"moments{i}", [P, BLOCKS, 2]) for i in range(2)]
        shift = [sb(f"shift{i}", [P, BLOCKS]) for i in range(2)]
        var_eps = [sb(f"var_eps{i}", [P, BLOCKS]) for i in range(2)]
        rstd = [sb(f"rstd{i}", [P, BLOCKS]) for i in range(2)]
        select_f32 = y0[0:SPREAD, 0:STATES, 0:P]
        minus_f32 = y0[0:SPREAD, STATES:STATES + 2, 0:LOW]
        dw_all = h[:, :, :, :].rearrange("p a b c -> p (a b c)")[:, 0:TAPS * INNER].rearrange("p (a b) -> p a b", a=TAPS)
        fc1_t = decay[:, 0, 0, 0:INNER]
        edge_scale = decay[0:TAPS + 1, 1, 0, 0:INNER]
        fc2_b_in = c_rows[:, 0, 0:1]

        b_bank = [ps(f"b_bank{i}", [P, WIN]) for i in range(2)]
        u_bank = [ps(f"u_bank{a}", [P, WIN]) for a in range(HALVES)]
        y_bank = ps("y_bank", [P, BLOCKS, INNER])
        post_bank = ps("post_bank", [P, WIN])
        pre_bank = ps("pre_bank", [P, WIN])
        z_banks = [post_bank, pre_bank]

        s_const = sem("constants_loaded")
        s_setup_dve = sem("setup_vector")
        s_setup_act = sem("setup_scalar")
        s_setup_pe = sem("setup_tensor")
        s_halo = [sem(f"halo{i}_loaded") for i in range(2)]
        s_xi_in = sem("xi_window_loaded")
        s_z_in = sem("z_window_loaded")
        s_x_in = sem("x_window_loaded")
        s_xi_st = sem("xi_stored")
        s_z_st = sem("z_stored")
        s_out_st = sem("output_stored")
        s_b = sem("b_broadcast")
        s_cst = sem("c_stored")
        s_c = [sem(f"c_pair{i}_loaded") for i in range(C_PAIRS)]
        s_decay = sem("decay_ready")
        s_u1 = sem("u1_ready")
        s_u0 = sem("u0_ready")
        s_h1 = sem("h1_ready")
        s_h = sem("h_ready")
        s_carry = sem("carry_saved")
        s_hc = sem("hc_ready")
        s_y = sem("y_added")
        s_skip = sem("skip_ready")
        s_skip_y = sem("skip_added")
        s_y0 = sem("y0_saved")
        s_yt = sem("y_total_ready")
        s_low = sem("low_ranks_ready")
        s_high = sem("part_high_ready")
        s_lowr = sem("low_rows_copied")
        s_sub = sem("part_subtracted")
        s_mid = sem("part_mid_ready")
        s_parts = sem("parts_ready")
        s_dtp = sem("dt_projected")
        s_lin = sem("dt_positive_part_ready")
        s_abs = sem("dt_abs_ready")
        s_e = sem("dt_exp_ready")
        s_ln = sem("dt_log_ready")
        s_dt = sem("dt_ready")
        s_dtx = sem("dtx_ready")
        s_conv = sem("conv_ready")
        s_hid = sem("hidden_ready")
        s_xip = sem("xi_projected")
        s_zp = sem("z_projected")
        s_xia = sem("xi_ready")
        s_za = sem("z_ready")
        s_stat = [sem("norm1_stats"), sem("norm2_stats")]
        s_mom = [sem("norm1_moments"), sem("norm2_moments")]
        s_ve = [sem("norm1_var_eps"), sem("norm2_var_eps")]
        s_rstd = [sem("norm1_rstd"), sem("norm2_rstd")]
        s_shift = [sem("norm1_shift"), sem("norm2_shift")]
        s_norm = [sem("norm1_done"), sem("norm2_done")]
        s_t1 = sem("norm1_transposed")
        s_g = sem("norm1_affine_done")
        s_gz = sem("gated_ready")
        s_op = sem("out_projected")
        s_o = sem("out_projection_copied")
        s_t2 = sem("norm2_transposed")
        s_ot = sem("norm2_transposed_copied")
        s_fc2 = sem("fc2_ready")
        s_res = sem("result_ready")

        constants = [
            (ident[:, :], d["ident"]),
            (select_f32, d["select"].rearrange("r (j p) -> r j p", p=P)),
            (minus_f32, d["minus"].rearrange("r (i m) -> r i m", m=LOW)),
            (dw_all, d["dw_rep"].rearrange("p (t n) -> p t n", t=TAPS)),
            (fc1_t, d["fc1_t"]),
            (edge_w[:, :], d["edge_w"]),
            (edge_scale, d["edge_scale"]),
            (in_w[:, :, :], d["in_w_t"].rearrange("(a p) n -> p a n", p=P)),
            (in_b[:, :, :], d["in_b"].rearrange("p (k a) -> p k a", k=2)),
            (A[:, :, :, :], d["A_log"].rearrange("p (k a n) -> p k a n", k=DIRS, a=HALVES)),
            (D[:, :, :], d["Ds"].rearrange("p (k a) -> p k a", k=DIRS)),
            (norm1_w[:, :], d["norm1_w"]),
            (norm1_b[:, :], d["norm1_b"]),
            (norm2_w[:, :], d["norm2_w"]),
            (norm2_b[:, :], d["norm2_b"]),
            (out_w[:, :, :], d["out_w_t"].rearrange("(a p) n -> p a n", p=P)),
            (out_b[:, :], d["out_b"]),
            (fc2_w[:, :, :], d["fc2_w_t"].rearrange("(a p) n -> p a n", p=P)),
            (fc2_b_in, d["fc2_b"]),
        ]
        SETUP_DVE = 10

        block = ctx.enter_context(nc.Block())

        @block.sync
        def _(sp):
            for where, what in constants:
                sp.dma_start(where, what).then_inc(s_const, 16)

            def ahead(*values):
                for v in values:
                    if isinstance(v, bass.AP):
                        sp.lower_ap_dma(v)
                    elif not isinstance(v, int):
                        sp.lower_val(v)

            def load_pre(q, b, hw, par):
                top, bottom = hw == 0, hw == PRES - 1
                inner = x_halo[par][:, :, 1:W + 1]
                if top:
                    pieces = [(0, 1, None), (1, ROWS + 2, 0)]
                elif bottom:
                    pieces = [(ROWS + 1, ROWS + 2, None), (0, ROWS + 1, hw * ROWS - 1)]
                else:
                    pieces = [(0, 2, hw * ROWS - 1), (2, ROWS + 2, hw * ROWS + 1)]
                src = [d["zero_row"].rearrange("p (r w) -> p r w", r=1) if row is None
                       else d["x"][b, :, row:row + hi - lo, :] for lo, hi, row in pieces]
                ahead(q - 1, *src)
                wait(sp, s_conv, q - 1)
                if isinstance(q, int) and q == 0:
                    sp.wait_ge(s_setup_dve, SETUP_DVE)
                for (lo, hi, _), rows in zip(pieces, src):
                    sp.dma_start(inner[:, lo:hi, :], rows).then_inc(s_halo[par], 16)
                sp.dma_start(edge_rows[par][:, :], d["edge_rows"][hw]).then_inc(s_halo[par], 16)

            def store_pre(q, b, hw):
                tok = slice(hw * HALF, (hw + 1) * HALF)
                xi_to, z_to = xi_dram[b, :, :, tok], z_dram[b, :, :, tok]
                ahead(q + 1, xi_to, z_to)
                wait(sp, s_xia, q + 1)
                sp.dma_start(xi_to, xi_out[:, :, :]).then_inc(s_xi_st, 16)
                wait(sp, s_za, q + 1)
                sp.dma_start(z_to, z_out[:, :, :]).then_inc(s_z_st, 16)

            def load_window(s1, b, k, win, par, skips=0):
                src = xi_dram[b, :, :, win * WIN:(win + 1) * WIN]
                stored = 16 * (b * PRES + 2 * win + 2)
                ahead(skips, stored, s1 - 1, 2 * s1, 2 * (s1 - 1), src)
                wait(sp, s_skip, skips)
                wait(sp, s_xi_st, stored)
                wait(sp, s_dtx, 2 * (s1 - 1))
                wait(sp, s_low, s1 - 1)
                wait(sp, s_lin, 2 * s1)
                sp.dma_start(xi[par][:, :, :], src).then_inc(s_xi_in, 16)
                sp.dma_start(low_w[:, :, :], d["low_w"][k].rearrange("(a p) n -> p a n", p=P)).then_inc(s_xi_in, 16)
                sp.dma_start(dt_w[DT_AT:LOW, :], d["dt_w_t"][k]).then_inc(s_xi_in, 16)
                sp.dma_start(dt_b[:, :], d["dt_b"][k]).then_inc(s_xi_in, 16)

            def load_z(p, b, win):
                src = z_dram[b, :, :, win * WIN:(win + 1) * WIN]
                stored = 16 * (b * PRES + 2 * win + 2)
                ahead(2 * p, stored, src)
                wait(sp, s_gz, 2 * p)
                wait(sp, s_z_st, stored)
                sp.dma_start(z_in[:, :, :], src).then_inc(s_z_in, 16)

            def load_x(p, b, win):
                src = x_flat[b, :, win * WIN:(win + 1) * WIN]
                ahead(p, src)
                wait(sp, s_res, p)
                sp.dma_start(x_in[:, :], src).then_inc(s_x_in, 16)

            def store_out(p, b, win):
                to = out_flat[b, :, win * WIN:(win + 1) * WIN]
                ahead(p + 1, to)
                wait(sp, s_res, p + 1)
                sp.dma_start(to, result[:, :]).then_inc(s_out_st, 16)

            load_pre(0, 0, 0, 0)
            load_pre(1, 0, 1, 1)
            for hw in range(PRES):
                if hw + 2 < PRES:
                    load_pre(hw + 2, 0, hw + 2, hw % 2)
                store_pre(hw, 0, hw)
            load_window(0, 0, 0, 0, 0)

            def image(b, first, last):
                for i in range(STEPS):
                    k, w = divmod(i, WINS)
                    s = b * STEPS + i
                    q = (b + 1) * PRES + i
                    skips = b * WINS + max(0, i - WINS)
                    if i + 1 < STEPS:
                        k1, w1 = divmod(i + 1, WINS)
                        load_window(s + 1, b, k1, w1 if k1 == 0 else WINS - 1 - w1, (i + 1) % 2, skips)
                    elif not last:
                        load_window(s + 1, b + 1, 0, 0, 0, skips)
                    if k == 1 and w >= 1:
                        load_z(b * WINS + w - 1, b, WINS - w)
                    if k == 1 and w >= 2:
                        load_x(b * WINS + w - 2, b, WINS + 1 - w)
                    if not first and i == 0:
                        load_z(b * WINS - 1, b - 1, 0)
                    if not first and i < 2:
                        load_x(b * WINS - 2 + i, b - 1, 1 - i)
                    if not last:
                        load_pre(q, b + 1, i, i % 2)
                    if i == 0:
                        if not first:
                            store_pre(q - 1, b, PRES - 1)
                    elif not last:
                        store_pre(q - 1, b + 1, i - 1)
                    if k == 1 and w >= 2:
                        store_out(b * WINS + w - 2, b, WINS + 1 - w)
                    if not first and i < 2:
                        store_out(b * WINS - 2 + i, b - 1, 1 - i)

            image(0, True, False)
            with sp.Fori(1, IMAGES - 1) as b:
                image(b, False, False)
            image(IMAGES - 1, False, True)
            end = IMAGES * WINS
            load_z(end - 1, IMAGES - 1, 0)
            for p in (end - 2, end - 1):
                load_x(p, IMAGES - 1, end - 1 - p)
                store_out(p, IMAGES - 1, end - 1 - p)
            sp.wait_ge(s_xi_st, 16 * IMAGES * PRES)
            sp.wait_ge(s_z_st, 16 * IMAGES * PRES)
            sp.wait_ge(s_out_st, 16 * end)

        @block.tensor
        def _(pe):
            mm = nc.tensor.matmul

            def turn(out, in_, start):
                return mm(out, in_, ident[:, :], is_transpose=True, start=start, stop=True, skip_group_check=True)

            pe.wait_ge(s_const, 16 * len(constants))
            for a in range(HALVES):
                last = mm(post_bank[:, 0:1], fc2_w[:, a, :], norm2_b[:, a:a + 1], start=(a == 0), stop=(a == HALVES - 1))
            last.then_inc(s_setup_pe, 1)

            def conv(q, par, lo, hi, bank=pre_bank):
                for i in range(lo, hi):
                    a, tap = divmod(i, TAPS + 1)
                    out = bank[:, a * HALF:(a + 1) * HALF]
                    if tap < TAPS:
                        dy, dx = divmod(tap, 3)
                        last = mm(out, conv_w[:, tap, a * P:(a + 1) * P], x_halo[par][:, dy:dy + ROWS, dx:dx + W],
                                  start=(tap == 0), stop=False)
                    else:
                        last = mm(out, edge_w[:, a * P:(a + 1) * P], edge_rows[par][:, :], start=False, stop=True)
                if hi == HALVES * (TAPS + 1):
                    last.then_inc(s_conv, 1)

            def in_proj(bank, base, a, done):
                out = bank[:, a * HALF:(a + 1) * HALF]
                cols = slice(base + a * P, base + (a + 1) * P)
                for c in range(HALVES):
                    last = mm(out, in_w[:, c, cols], hidden[:, c, :], start=(c == 0), stop=(c == HALVES - 1))
                if a == HALVES - 1:
                    last.then_inc(done, 1)

            def low_ranks(s1, par):
                pe.wait_ge(s_xi_in, 64 * (s1 + 1))
                for c in range(HALVES):
                    last = mm(pre_bank[0:LOW, :], low_w[:, c, :], xi[par][:, c, :], start=(c == 0), stop=(c == HALVES - 1))
                last.then_inc(s_low, 1)

            def subtract(s1, i):
                if i == 0:
                    pe.wait_ge(s_lowr, s1 + 1)
                    pe.wait_ge(s_high, s1 + 1)
                else:
                    pe.wait_ge(s_mid, s1 + 1)
                part = part_high if i == 0 else part_mid
                mm(pre_bank[0:LOW, :], minus[:, i, :], part[:, :], start=False, stop=True,
                   skip_group_check=True).then_inc(s_sub, 1)

            def dt_proj(s1, a):
                if a == 0:
                    pe.wait_ge(s_parts, s1 + 1)
                else:
                    pe.wait_ge(s_lin, 2 * s1 + 1)
                mm(pre_bank[:, :], dt_w[DT_AT:LOW, a * P:(a + 1) * P], low_rows[DT_AT:LOW, :],
                   start=True, stop=True).then_inc(s_dtp, 1)

            def spread_b(s, n, par):
                if n == 0:
                    pe.wait_ge(s_parts, s + 1)
                wait(pe, s_u0, s * STATES + n - 1)
                mm(b_bank[n % 2][:, :], select[:, n, :], parts[par][:, :], start=True, stop=True).then_inc(s_b, 1)

            def add_y(s, n, left, st):
                pe.wait_ge(s_hc, s * STATES + n + 1)
                if n == 0:
                    if left == 0:
                        pe.wait_ge(s_y0, st.kept_before + 1)
                    elif left == 1:
                        pe.wait_ge(s_yt, st.p1 + 1)
                for a in range(HALVES):
                    for j in range(BLOCKS):
                        last = turn(y_bank[:, j, a * P:(a + 1) * P], hc[:, n % RING, a, j * P:(j + 1) * P],
                                    start=(n == 0 and a == 0 and j % 2 == 0))
                last.then_inc(s_y, 1)

            def add_skip(count):
                pe.wait_ge(s_skip, count)
                for a in range(HALVES):
                    for j in range(BLOCKS):
                        last = turn(y_bank[:, j, a * P:(a + 1) * P], skip[:, a, j * P:(j + 1) * P], start=False)
                last.then_inc(s_skip_y, 1)

            def turn1(p, a):
                if a == 0:
                    pe.wait_ge(s_norm[0], p + 1)
                else:
                    pe.wait_ge(s_g, 2 * p + 1)
                for j in range(BLOCKS):
                    last = turn(post_bank[:, j * P:(j + 1) * P], yt[:, j, a * P:(a + 1) * P], start=True)
                last.then_inc(s_t1, 1)

            def out_proj(p, j):
                if j % 2 == 0:
                    pe.wait_ge(s_gz, 2 * p + j // 2 + 1)
                if j == 2:
                    pe.wait_ge(s_o, 2 * p + 1)
                out = post_bank[:, j % 2 * INNER:(j % 2 + 1) * INNER]
                for c in range(HALVES):
                    mm(out, gated[:, c, j * P:(j + 1) * P], out_w[:, c, :], start=(c == 0), stop=False)
                last = mm(out, ones[:, :], out_b[:, :], start=False, stop=True)
                if j % 2 == 1:
                    last.then_inc(s_op, 1)

            def turn2(p, a):
                if a == 0:
                    pe.wait_ge(s_norm[1], p + 1)
                else:
                    pe.wait_ge(s_ot, 2 * p + 1)
                for j in range(BLOCKS):
                    last = turn(post_bank[:, j * P:(j + 1) * P], o[:, j, a * P:(a + 1) * P], start=True)
                last.then_inc(s_t2, 1)

            def fc2(p):
                pe.wait_ge(s_ot, 2 * p + 2)
                for c in range(HALVES):
                    last = mm(post_bank[:, :], fc2_w[:, c, :], o_t[:, c, :], start=(c == 0), stop=(c == HALVES - 1))
                last.then_inc(s_fc2, 1)

            pe.wait_ge(s_setup_dve, SETUP_DVE)
            pe.wait_ge(s_setup_act, 3)

            def conv_alone(q, par):
                pe.wait_ge(s_halo[par], halo_count(q, par))
                wait(pe, s_hid, q - 1)
                conv(q, par, 0, HALVES * (TAPS + 1), u_bank[par])

            def pre_alone(q, par):
                if not isinstance(q, int) or q + 1 < PRES:
                    conv_alone(q + 1, 1 - par)
                pe.wait_ge(s_hid, q + 1)
                wait(pe, s_xia, q - 1)
                wait(pe, s_za, q - 1)
                for a in range(HALVES):
                    in_proj(b_bank[par], 0, a, s_xip)
                for a in range(HALVES):
                    in_proj(z_banks[par], INNER, a, s_zp)

            conv_alone(0, 0)
            pre_alone(0, 0)
            pre_alone(1, 1)
            with pe.Fori(1, PRES // 2 - 1) as i:
                pre_alone(2 * i, 0)
                pre_alone(2 * i + 1, 1)
            pre_alone(PRES - 2, 0)
            pre_alone(PRES - 1, 1)
            pe.wait_ge(s_xia, PRES)
            pe.wait_ge(s_za, PRES)
            low_ranks(0, 0)
            subtract(0, 0)
            subtract(0, 1)
            dt_proj(0, 0)
            dt_proj(0, 1)
            spread_b(0, 0, 0)

            def project(st, n):
                if st.last:
                    return
                s1, par = st.s + 1, 1 - st.parity
                if n == 1:
                    if st.finish:
                        pe.wait_ge(s_xia, st.pre_index)
                    low_ranks(s1, par)
                if n in (2, 3):
                    subtract(s1, n - 2)
                if n in (4, 5):
                    dt_proj(s1, n - 4)

            def step(st):
                s, par, nxt = st.s, st.parity, 1 - st.parity
                for n in range(STATES):
                    if n + 1 < STATES:
                        spread_b(s, n + 1, par)
                    elif not st.last:
                        spread_b(s + 1, 0, nxt)
                    if n != 2 or not st.post1:
                        project(st, n)
                    if n == 3 and st.post2:
                        out_proj(st.p2, 1)
                    if n >= LAG:
                        add_y(s, n - LAG, st.left, st)
                    elif not st.first:
                        add_y(s - 1, STATES - LAG + n, None, st)
                    if n == 2 and st.post1:
                        project(st, n)
                    if n == 6 and st.k == 1:
                        add_skip(st.b * WINS + st.w + 1)
                    if st.pre:
                        if n == CONV_SLOTS[0]:
                            pe.wait_ge(s_halo[par], halo_count(st.pre_index, par))
                            pe.wait_ge(s_lin, 2 * (s + 1) + 2)
                        if n in CONV_SLOTS:
                            i = n - CONV_SLOTS[0]
                            conv(st.pre_index, par, CONV_CUTS[i], CONV_CUTS[i + 1])
                        if n == 13:
                            pe.wait_ge(s_hid, st.pre_index + 1)
                        if n in (13, 14):
                            in_proj(pre_bank, 0, n - 13, s_xip)
                    if st.post2:
                        if n == 2:
                            if st.finish:
                                pe.wait_ge(s_za, st.pre_index)
                            out_proj(st.p2, 0)
                        if n in (4, 5):
                            out_proj(st.p2, n - 2)
                        if n == 10:
                            pe.wait_ge(s_o, 2 * st.p2 + 2)
                            turn2(st.p2, 0)
                        if n == 11:
                            turn2(st.p2, 1)
                        if n == 12:
                            fc2(st.p2)
                    if st.post1:
                        if n == 13:
                            if st.post2:
                                pe.wait_ge(s_res, st.p2 + 1)
                            elif st.finish:
                                pe.wait_ge(s_za, st.pre_index)
                            turn1(st.p1, 0)
                        if n == 14:
                            turn1(st.p1, 1)
                    if st.pre and n == 15:
                        if st.post1:
                            pe.wait_ge(s_g, 2 * st.p1 + 2)
                        elif st.post2:
                            pe.wait_ge(s_res, st.p2 + 1)
                        wait(pe, s_za, st.pre_index)
                        for a in range(HALVES):
                            in_proj(post_bank, INNER, a, s_zp)

            walk(pe, step)
            end = IMAGES * WINS
            s_end = IMAGES * STEPS
            for n in range(STATES - LAG, STATES):
                add_y(s_end - 1, n, None, None)
            for p in (end - 2, end - 1):
                if p == end - 1:
                    pe.wait_ge(s_res, p)
                    turn1(p, 0)
                    turn1(p, 1)
                for j in range(BLOCKS):
                    out_proj(p, j)
                pe.wait_ge(s_o, 2 * p + 2)
                turn2(p, 0)
                turn2(p, 1)
                fc2(p)

        @block.scalar
        def _(act):
            run = nc.scalar.activation
            nc.scalar.preload_act_table_set(LN_EXP_SET)
            act.wait_ge(s_const, 16 * len(constants))
            run(A[:, :, :, :], A[:, :, :, :], ACT.Exp).then_inc(s_setup_act, 1)
            nc.scalar.copy(select[:, :, :], select_f32).then_inc(s_setup_act, 1)
            nc.scalar.copy(minus[:, :, :], minus_f32).then_inc(s_setup_act, 1)

            def silu_in(to, bank, k, done):
                for a in range(HALVES):
                    last = run(to[:, a, :], bank[:, a * HALF:(a + 1) * HALF], ACT.Silu, bias=in_b[:, k, a:a + 1])
                last.then_inc(done, 1)

            def silu_hidden(q, bank=pre_bank):
                act.wait_ge(s_conv, q + 1)
                wait(act, s_zp, q)
                run(hidden[:, :, :], bank[:, :].rearrange("p (a n) -> p a n", a=HALVES), ACT.Silu).then_inc(s_hid, 1)

            def silu_xi_z(q, xi_bank=pre_bank, z_bank=post_bank):
                act.wait_ge(s_xip, q + 1)
                wait(act, s_xi_st, 16 * q)
                silu_in(xi_out, xi_bank, 0, s_xia)
                act.wait_ge(s_zp, q + 1)
                wait(act, s_z_st, 16 * q)
                silu_in(z_out, z_bank, 1, s_za)

            def split_high(s1, par):
                act.wait_ge(s_low, s1 + 1)
                wait(act, s_cst, 16 * s1)
                wait(act, s_dtp, 2 * s1)
                nc.scalar.copy(low_rows[C_AT:LOW, :], pre_bank[C_AT:LOW, :]).then_inc(s_lowr, 1)
                wait(act, s_sub, 2 * s1)
                nc.scalar.copy(part_high[:, :], pre_bank[0:SPREAD, :]).then_inc(s_high, 1)
                act.wait_ge(s_lowr, s1 + 1)
                for i in range(C_PAIRS):
                    wait(act, s_c[i], 32 * (s1 - 1))
                nc.scalar.dma_start(c_dram[par], low_rows[C_AT:C_AT + STATES, :]).then_inc(s_cst, 16)

            def split_mid(s1):
                act.wait_ge(s_sub, 2 * s1 + 1)
                nc.scalar.copy(part_mid[:, :], pre_bank[0:SPREAD, :]).then_inc(s_mid, 1)

            def split_low(s1, par):
                act.wait_ge(s_sub, 2 * s1 + 2)
                nc.scalar.copy(parts[par][:, :], pre_bank[0:SPREAD, :]).then_inc(s_parts, 1)

            def load_c(s1, par, m):
                act.wait_ge(s_cst, 16 * (s1 + 1))
                wait(act, s_hc, s1 * STATES + 2 * m + 2 - C_RING)
                at = 2 * (m % C_PAIRS)
                src = c_dram[par:par + 1, 2 * m:2 * m + 2, :].broadcast_to((P, 2, WIN))
                nc.scalar.dma_start(c_rows[:, at:at + 2, :], src).then_inc(s_c[m % C_PAIRS], 16)

            def dt_linear(s1, a):
                act.wait_ge(s_dtp, 2 * s1 + a + 1)
                if a == 0:
                    wait(act, s_dt, s1)
                run(dt_exp[:, a, :], pre_bank[:, :], ACT.Abs, bias=dt_b[:, a:a + 1]).then_inc(s_abs, 1)
                run(dt_lin[:, a, :], pre_bank[:, :], ACT.Relu, bias=dt_b[:, a:a + 1]).then_inc(s_lin, 1)

            def dt_softplus(s1):
                act.wait_ge(s_abs, 2 * s1 + 2)
                run(dt_exp[:, :, :], dt_exp[:, :, :], ACT.Exp, scale=-1.0).then_inc(s_e, 1)
                act.wait_ge(s_e, s1 + 1)
                run(dt_exp[:, :, :], dt_exp[:, :, :], ACT.Ln, bias=1.0).then_inc(s_ln, 1)

            def decays(st, n):
                s = st.s
                if n == 0:
                    act.wait_ge(s_dt, s + 1)
                wait(act, s_h, s * STATES + n - RING + 1)
                for a in range(HALVES):
                    last = run(decay[:, n % RING, a, :], dt[st.parity][:, a, :], ACT.Exp, scale=A[:, st.k, a, n:n + 1])
                last.then_inc(s_decay, 1)

            def affine1(p, a):
                act.wait_ge(s_t1, 2 * p + a + 1)
                run(gated[:, a, :], post_bank[:, :], ACT.Identity, bias=norm1_b[:, a:a + 1],
                    scale=norm1_w[:, a:a + 1]).then_inc(s_g, 1)

            def copy_o(p, a):
                act.wait_ge(s_op, 2 * p + a + 1)
                nc.scalar.copy(o[:, 2 * a:2 * a + 2, :], post_bank[:, :].rearrange("p (j n) -> p j n", j=2)).then_inc(s_o, 1)

            def copy_ot(p, a):
                act.wait_ge(s_t2, 2 * p + a + 1)
                if a == 0:
                    wait(act, s_fc2, p)
                nc.scalar.copy(o_t[:, a, :], post_bank[:, :]).then_inc(s_ot, 1)

            def normalize(i, buf, p):
                act.wait_ge(s_shift[i], p + 1)
                for j in range(BLOCKS):
                    last = run(buf[:, j, :], buf[:, j, :], ACT.Identity, bias=shift[i][:, j:j + 1], scale=rstd[i][:, j:j + 1])
                last.then_inc(s_norm[i], 1)

            nc.scalar.preload_act_table_set(SILU_SET)
            silu_hidden(0, u_bank[0])
            silu_xi_z(0, b_bank[0], z_banks[0])
            with act.Fori(0, PRES // 2 - 1) as i:
                for par in (1, 0):
                    q = 2 * i + 2 - par
                    silu_hidden(q, u_bank[par])
                    silu_xi_z(q, b_bank[par], z_banks[par])
            silu_hidden(PRES - 1, u_bank[1])
            silu_xi_z(PRES - 1, b_bank[1], z_banks[1])
            nc.scalar.preload_act_table_set(LN_EXP_SET)
            act.wait_ge(s_setup_dve, SETUP_DVE)
            split_high(0, 0)
            split_mid(0)
            split_low(0, 0)
            load_c(0, 0, 0)
            dt_linear(0, 0)
            dt_linear(0, 1)
            dt_softplus(0)

            def step(st):
                s, par, nxt = st.s, st.parity, 1 - st.parity
                decays(st, 0)
                decays(st, 1)
                for n in range(STATES):
                    if n + 2 < STATES:
                        decays(st, n + 2)
                    if n % 2 == 0:
                        m = n // 2 + 1
                        if m < STATES // 2:
                            load_c(s, par, m)
                        elif not st.last:
                            load_c(s + 1, nxt, m - STATES // 2)
                    if n == 0 and st.finish:
                        nc.scalar.preload_act_table_set(SILU_SET)
                        silu_xi_z(st.pre_index - 1)
                        nc.scalar.preload_act_table_set(LN_EXP_SET)
                    if n == 2 and st.keep_y0:
                        act.wait_ge(s_y, s * STATES)
                        wait(act, s_yt, st.b * WINS)
                        nc.scalar.copy(y0[:, blocks_of(st.keep_window), :], y_bank[:, :, :]).then_inc(s_y0, 1)
                    if n in (3, 5) and st.post2:
                        copy_o(st.p2, (n - 3) // 2)
                    if not st.last:
                        if n == 1:
                            split_high(s + 1, nxt)
                        if n == 2:
                            split_mid(s + 1)
                        if n == 3:
                            split_low(s + 1, nxt)
                        if n == 4:
                            dt_linear(s + 1, 0)
                        if n == 5:
                            dt_linear(s + 1, 1)
                        if n == 6:
                            dt_softplus(s + 1)
                    if n == 4 and st.k == 1:
                        wait(act, s_skip_y, st.b * WINS + st.w)
                        act.wait_ge(s_xi_in, 64 * (s + 1))
                        for a in range(HALVES):
                            last = run(skip[:, a, :], xi[par][:, a, :], ACT.Copy, scale=D_sum[:, a:a + 1])
                        last.then_inc(s_skip, 1)
                    if st.post2:
                        if n == 9:
                            normalize(1, o, st.p2)
                        if n == 10:
                            copy_ot(st.p2, 0)
                        if n == 11:
                            copy_ot(st.p2, 1)
                    if st.post1 and n == 8:
                        normalize(0, yt, st.p1)
                    if st.pre and n == 12:
                        nc.scalar.preload_act_table_set(SILU_SET)
                        silu_hidden(st.pre_index)
                        nc.scalar.preload_act_table_set(LN_EXP_SET)
                    if st.post1 and n in (13, 14):
                        affine1(st.p1, n - 13)

            walk(act, step)
            end = IMAGES * WINS
            normalize(0, yt, end - 1)
            for p in (end - 2, end - 1):
                if p == end - 1:
                    affine1(p, 0)
                    affine1(p, 1)
                copy_o(p, 0)
                copy_o(p, 1)
                normalize(1, o, p)
                copy_ot(p, 0)
                copy_ot(p, 1)

        @block.vector
        def _(dve):
            V = nc.vector
            dve.wait_ge(s_const, 16 * len(constants))
            for x_rows in x_halo:
                V.memset(x_rows[:, :, :], 0.0).then_inc(s_setup_dve, 1)
            V.memset(ones[:, :], 1.0).then_inc(s_setup_dve, 1)
            V.memset(minus_half[:, :], -0.5).then_inc(s_setup_dve, 1)
            V.tensor_tensor(conv_w[:, :, :], dw_all, fc1_t.rearrange("p (t n) -> p t n", t=1).broadcast_to((P, TAPS, INNER)),
                            ALU.mult).then_inc(s_setup_dve, 1)
            V.tensor_tensor(edge_w[:, :], edge_w[:, :], edge_scale, ALU.mult).then_inc(s_setup_dve, 1)
            V.tensor_tensor(D_sum[:, :], D[:, 0, :], D[:, 1, :], ALU.add).then_inc(s_setup_dve, 1)
            dve.wait_ge(s_setup_act, 1)
            V.tensor_scalar(A[:, :, :, :], A[:, :, :, :], -1.0, None, ALU.mult).then_inc(s_setup_dve, 1)
            dve.wait_ge(s_setup_pe, 1)
            V.tensor_tensor(fc2_b[:, :], post_bank[:, 0:1], fc2_b_in, ALU.add).then_inc(s_setup_dve, 1)
            V.tensor_tensor(fc2_w[:, :, :], fc2_w[:, :, :],
                            norm2_w[:, :].rearrange("p (a n) -> p a n", n=1).broadcast_to((P, HALVES, DIM)),
                            ALU.mult).then_inc(s_setup_dve, 1)
            dve.wait_ge(s_setup_dve, SETUP_DVE)

            def dt_sum(s1, par):
                dve.wait_ge(s_ln, s1 + 1)
                dve.wait_ge(s_lin, 2 * s1 + 2)
                V.tensor_tensor(dt[par][:, :, :], dt_exp[:, :, :], dt_lin[:, :, :], ALU.add).then_inc(s_dt, 1)

            def norm_stats(i, src, p):
                for j in range(BLOCKS):
                    V.bn_stats(stats[i][:, j, :], src[:, j, :]).then_inc(s_stat[i], 1)

            def norm_moments(i, p):
                dve.wait_ge(s_stat[i], BLOCKS * (p + 1))
                V.memset(var_eps[i][:, :], EPS).then_inc(s_ve[i], 1)
                for j in range(BLOCKS):
                    V.bn_aggr(moments[i][:, j, :], stats[i][:, j, :]).then_inc(s_mom[i], 1)

            def norm_var(i, p):
                dve.wait_ge(s_ve[i], 2 * p + 1)
                dve.wait_ge(s_mom[i], BLOCKS * (p + 1))
                V.tensor_tensor(var_eps[i][:, :], var_eps[i][:, :], moments[i][:, :, 1], ALU.add).then_inc(s_ve[i], 1)

            def norm_shift(i, p):
                dve.wait_ge(s_rstd[i], p + 1)
                wait(dve, s_norm[i], p)
                V.scalar_tensor_tensor(out=shift[i][:, :], in0=moments[i][:, :, 0], scalar=-1.0, in1=rstd[i][:, :],
                                       op0=ALU.mult, op1=ALU.mult).then_inc(s_shift[i], 1)

            def total_y(s, p, window):
                dve.wait_ge(s_y, s * STATES)
                dve.wait_ge(s_skip_y, p + 1)
                wait(dve, s_t1, 2 * p)
                dve.wait_ge(s_y0, p + 1)
                V.tensor_tensor(yt[:, :, :], y_bank[:, :, :], y0[:, blocks_of(window), :],
                                ALU.add).then_inc(s_yt, 1)

            def finish_out(p):
                dve.wait_ge(s_fc2, p + 1)
                dve.wait_ge(s_x_in, 16 * (p + 1))
                wait(dve, s_out_st, 16 * p)
                V.scalar_tensor_tensor(out=result[:, :], in0=post_bank[:, :], scalar=fc2_b[:, 0:1], in1=x_in[:, :],
                                       op0=ALU.add, op1=ALU.add).then_inc(s_res, 1)

            dt_sum(0, 0)

            def step(st):
                s, par, nxt, k = st.s, st.parity, 1 - st.parity, st.k
                way = slice(None) if k == 0 else slice(WIN - 1, None, -1)
                end = WIN - 1 if k == 0 else 0

                def make_u(n, a, done):
                    V.tensor_tensor(u_bank[a][:, :], dtx[par][:, a, :], b_bank[n % 2][:, :], ALU.mult).then_inc(done, 1)

                def scan(n, a, done):
                    V.tensor_tensor_scan(h[:, n % RING, a, way], decay[:, n % RING, a, way], u_bank[a][:, way],
                                         0.0 if st.static_w == 0 else carry[:, n, a:a + 1],
                                         ALU.mult, ALU.add).then_inc(done, 1)

                def keep_carry(n, step_of):
                    dve.wait_ge(s_h, step_of * STATES + n + 1)
                    V.tensor_copy(carry[:, n - RING + 1:n + 1, :], h[:, :, :, end]).then_inc(s_carry, 1)

                kept = s * (STATES // RING - 1) + (st.b * DIRS + k) * (WINS - 1) + st.w
                for n in range(STATES):
                    count = s * STATES + n
                    if n == 0:
                        dve.wait_ge(s_dtx, HALVES * (s + 1))
                    dve.wait_ge(s_b, count + 1)
                    wait(dve, s_h1, count)
                    make_u(n, 1, s_u1)
                    wait(dve, s_h, count)
                    if n == 0 and st.static_w != 0:
                        keep_carry(STATES - 1, s - 1)
                    if n and n % RING == 0:
                        keep_carry(n - 1, s)
                    make_u(n, 0, s_u0)
                    if n == 9 and not st.last:
                        dt_sum(s + 1, nxt)
                    if st.post2:
                        if n == 7:
                            norm_moments(1, st.p2)
                        if n == 9:
                            norm_shift(1, st.p2)
                    if st.post1:
                        if n == 5:
                            norm_moments(0, st.p1)
                        if n == 7:
                            norm_shift(0, st.p1)
                    dve.wait_ge(s_u1, count + 1)
                    dve.wait_ge(s_decay, count + 1)
                    wait(dve, s_hc, count - RING + 1)
                    wait(dve, s_carry, kept + n // RING)
                    scan(n, 1, s_h1)
                    dve.wait_ge(s_u0, count + 1)
                    scan(n, 0, s_h)
                    if st.post1:
                        if n == 2:
                            total_y(s, st.p1, st.p1_window)
                        if n == 4:
                            dve.wait_ge(s_yt, st.p1 + 1)
                            norm_stats(0, yt, st.p1)
                        if n == 5:
                            norm_var(0, st.p1)
                    if st.post2:
                        if n == 6:
                            dve.wait_ge(s_o, 2 * st.p2 + 2)
                            norm_stats(1, o, st.p2)
                        if n == 7:
                            norm_var(1, st.p2)
                        if n == 12:
                            finish_out(st.p2)

            walk(dve, step)
            end = IMAGES * WINS
            total_y(IMAGES * STEPS, end - 1, 0)
            dve.wait_ge(s_yt, end)
            norm_stats(0, yt, end - 1)
            norm_moments(0, end - 1)
            norm_var(0, end - 1)
            norm_shift(0, end - 1)
            for p in (end - 2, end - 1):
                dve.wait_ge(s_o, 2 * p + 2)
                norm_stats(1, o, p)
                norm_moments(1, p)
                norm_var(1, p)
                norm_shift(1, p)
                finish_out(p)

        @block.gpsimd
        def _(pool):
            G = nc.gpsimd

            def inverse_root(i, p):
                pool.wait_ge(s_ve[i], 2 * p + 2)
                G.tensor_tensor(rstd[i][:, :], var_eps[i][:, :], minus_half[:, :], ALU.pow).then_inc(s_rstd[i], 1)

            def gate(p, part):
                if part == 0:
                    pool.wait_ge(s_g, 2 * p + 2)
                    pool.wait_ge(s_z_in, 16 * (p + 1))
                tok = slice(part * HALF, (part + 1) * HALF)
                G.tensor_tensor(gated[:, :, tok], gated[:, :, tok], z_in[:, :, tok], ALU.mult).then_inc(s_gz, 1)

            def dt_times_x(s1, par, a):
                if a == 0:
                    pool.wait_ge(s_xi_in, 64 * (s1 + 1))
                    pool.wait_ge(s_dt, s1 + 1)
                G.tensor_tensor(dtx[par][:, a, :], dt[par][:, a, :], xi[par][:, a, :], ALU.mult).then_inc(s_dtx, 1)

            pool.wait_ge(s_setup_dve, SETUP_DVE)
            for a in range(HALVES):
                dt_times_x(0, 0, a)

            def step(st):
                for n in range(STATES):
                    count = st.s * STATES + n
                    pool.wait_ge(s_h, count + 1)
                    if n % 2 == 0:
                        pool.wait_ge(s_c[n // 2 % C_PAIRS], 16 * (2 * st.s + n // C_RING + 1))
                    wait(pool, s_y, count - RING + 1)
                    G.tensor_tensor(hc[:, n % RING, :, :], h[:, n % RING, :, :],
                                    c_rows[:, n % C_RING, :].rearrange("p (a n) -> p a n", a=1).broadcast_to((P, HALVES, WIN)),
                                    ALU.mult).then_inc(s_hc, 1)
                    if st.post1 and n == 5:
                        inverse_root(0, st.p1)
                    if st.post2 and n == 7:
                        inverse_root(1, st.p2)
                    if not st.last and n in (10, 11):
                        dt_times_x(st.s + 1, 1 - st.parity, n - 10)
                    if st.post2 and n == 1:
                        gate(st.p2, 1)
                    if st.post1 and n == 14:
                        gate(st.p1, 0)

            walk(pool, step)
            end = IMAGES * WINS
            inverse_root(0, end - 1)
            for p in (end - 2, end - 1):
                if p == end - 1:
                    gate(p, 0)
                gate(p, 1)
                inverse_root(1, p)


def edge_table():
    inside = np.ones((PRES, TAPS + 1, ROWS, W), np.float32)
    for tap in range(TAPS):
        dy, dx = divmod(tap, 3)
        if dy == 0:
            inside[0, tap, 0, :] = 0
        if dy == 2:
            inside[PRES - 1, tap, ROWS - 1, :] = 0
        if dx == 0:
            inside[:, tap, :, 0] = 0
        if dx == 2:
            inside[:, tap, :, W - 1] = 0
    return inside.reshape(PRES, TAPS + 1, HALF)


def select_table():
    table = np.zeros((SPREAD, STATES, P), np.float32)
    for r in range(SPREAD):
        table[r, r % STATES, :] = 1
    return table.reshape(SPREAD, STATES * P)


def minus_table():
    table = np.zeros((SPREAD, 2, LOW), np.float32)
    for i in range(2):
        for r in range((i + 1) * STATES, SPREAD):
            table[r, i, r] = -1
    return table.reshape(SPREAD, 2 * LOW)


def kernel(**inputs):
    import concourse.bacc as bacc
    from concourse.bass_utils import run_bass_kernel_spmd

    get = {n.removeprefix("L0_conv_"): np.asarray(a) for n, a in inputs.items()}
    xw = get["x_proj_w"]
    B, C = xw[:, RANK:RANK + STATES, :], xw[:, RANK + STATES:, :]
    gap = np.zeros((DIRS, C_AT - SPREAD, INNER), np.float32)
    one_row = np.ones((1, INNER), np.float32)
    arrays = {
        "x": get["x"],
        "ident": np.eye(P, dtype=np.float32),
        "select": select_table(),
        "minus": minus_table(),
        "edge_rows": edge_table(),
        "zero_row": np.zeros((P, W), np.float32),
        "fc1_t": get["fc1_w"].T,
        "dw_rep": np.broadcast_to(get["dw_w"].reshape(INNER, TAPS).T.reshape(1, TAPS * INNER), (P, TAPS * INNER)),
        "edge_w": np.concatenate([get["dw_w"].reshape(INNER, TAPS).T, get["dw_b"].reshape(1, INNER)]),
        "edge_scale": np.concatenate([np.broadcast_to(get["fc1_b"].reshape(1, INNER), (TAPS, INNER)), one_row]),
        "in_w_t": get["in_proj_w"].T,
        "in_b": get["in_proj_b"].reshape(2 * HALVES, P).T,
        "low_w": np.concatenate([B, B, B, gap, C, gap, xw[:, :RANK, :]], axis=1).transpose(0, 2, 1),
        "dt_w_t": get["dt_proj_w"].transpose(0, 2, 1),
        "dt_b": get["dt_proj_b"].reshape(DIRS, HALVES, P).transpose(0, 2, 1),
        "A_log": get["A_log"].reshape(DIRS, HALVES, P, STATES).transpose(2, 0, 1, 3).reshape(P, -1),
        "Ds": get["Ds"].reshape(DIRS, HALVES, P).transpose(2, 0, 1).reshape(P, -1),
        "norm1_w": get["out_norm_w"].reshape(HALVES, P).T,
        "norm1_b": get["out_norm_b"].reshape(HALVES, P).T,
        "norm2_w": get["norm_w"].reshape(HALVES, P).T,
        "norm2_b": get["norm_b"].reshape(HALVES, P).T,
        "out_w_t": get["out_proj_w"].T,
        "out_b": get["out_proj_b"].reshape(1, INNER),
        "fc2_w_t": get["fc2_w"].T,
        "fc2_b": get["fc2_b"].reshape(DIM, 1),
    }
    nc = bacc.Bacc("TRN2", target_bir_lowering=False, num_devices=1)
    feed, d = {}, {}
    for name, a in arrays.items():
        a = np.ascontiguousarray(a)
        feed[f"in_{name}"] = a
        d[name] = nc.dram_tensor(f"in_{name}", a.shape, mybir.dt.from_np(a.dtype), kind="ExternalInput").ap()
    d["out"] = nc.dram_tensor("out_0", (IMAGES, DIM, H, W), F32, kind="ExternalOutput").ap()
    build(nc, d)
    r = run_bass_kernel_spmd(nc, [feed], core_ids=[0])
    return r.results[0]["out_0"]
```
